# Optimizing a Trainium2 kernel written in Bass

```python
import numpy as np
import jax
import jax.numpy as jnp

def _softmax(x, axis=-1):
    return jax.nn.softmax(x, axis=axis)
def _gelu(x):
    return jax.nn.gelu(x, approximate=True)
def _silu(x):
    return jax.nn.silu(x)
def _sigmoid(x):
    return jax.nn.sigmoid(x)
def _layernorm(x, axis=-1, eps=1e-5):
    m = jnp.mean(x, axis=axis, keepdims=True)
    v = jnp.var(x, axis=axis, keepdims=True)
    return (x - m) / jnp.sqrt(v + eps)
def _scatter_add(tgt, idx, src, axis=0):
    return tgt.at[idx].add(src)
def _segment_sum(src, seg, n):
    return jax.ops.segment_sum(src, seg, n)

kernel_name = 'mk_conv_preact_d1_conv_nhwc512_f4847f'

def setup_inputs(seed: int = 0):
    np.random.seed(seed)
    _w = jnp.asarray
    def _rec_inputs():
        import jax
        import jax.numpy as jnp
        _gk = jax.random.key(seed)
        x = -0.000125 + 0.9999 * jax.random.normal(jax.random.fold_in(_gk, 1), (16, 64, 64, 512), jnp.float32)
        return x
    x = _rec_inputs()
    def _L0_conv_setup():
        import jax, jax.numpy as jnp
        import numpy as np
        B, H, W, C, K = (16, 64, 64, 512, 128)
        EPS_L1 = 1e-09
        EPS_BN = 1e-05
        LEAK = 0.2
        key = jax.random.key(seed)
        ks = jax.random.split(key, 4)
        x = jax.random.normal(ks[0], (B, H, W, C), dtype=jnp.float32)
        Wq = jax.random.normal(ks[1], (C, C), dtype=jnp.float32) * (1.0 / np.sqrt(C))
        Mk = jax.random.normal(ks[2], (K, C), dtype=jnp.float32) * (1.0 / np.sqrt(C))
        Mv = jax.random.normal(ks[3], (C, K), dtype=jnp.float32) * (1.0 / np.sqrt(K))
        return {'x': x, 'Wq': Wq, 'bq': jnp.zeros((C,), jnp.float32), 'Mk': Mk, 'Mv': Mv, 'bv': jnp.zeros((C,), jnp.float32), 'gamma': jnp.ones((C,), jnp.float32), 'beta': jnp.zeros((C,), jnp.float32)}
    _L0_conv_all = _L0_conv_setup()
    _L0_conv_in = {k: v for k, v in _L0_conv_all.items() if k in ('Wq', 'bq', 'Mk', 'Mv', 'bv', 'gamma', 'beta', )}
    del _L0_conv_all

    return {
        "x": x,
        "L0_conv_Wq": _L0_conv_in["Wq"],
        "L0_conv_bq": _L0_conv_in["bq"],
        "L0_conv_Mk": _L0_conv_in["Mk"],
        "L0_conv_Mv": _L0_conv_in["Mv"],
        "L0_conv_bv": _L0_conv_in["bv"],
        "L0_conv_gamma": _L0_conv_in["gamma"],
        "L0_conv_beta": _L0_conv_in["beta"],
    }

def reference(x, L0_conv_Wq, L0_conv_bq, L0_conv_Mk, L0_conv_Mv, L0_conv_bv, L0_conv_gamma, L0_conv_beta):
    import jax
    import jax.numpy as jnp
    def _L0_conv_ref(x, Wq, bq, Mk, Mv, bv, gamma, beta):
        import jax, jax.numpy as jnp
        import numpy as np
        B, H, W, C, K = (16, 64, 64, 512, 128)
        EPS_L1 = 1e-09
        EPS_BN = 1e-05
        LEAK = 0.2
        b, h, w, c = x.shape
        idn = x
        q = jnp.einsum('bhwc,dc->bhwd', x, Wq) + bq
        qn = q.reshape(b, h * w, c)
        attn = jnp.einsum('bnc,kc->bnk', qn, Mk)
        attn = jax.nn.softmax(attn, axis=1)
        attn = attn / (EPS_L1 + attn.sum(axis=2, keepdims=True))
        out = jnp.einsum('bnk,ck->bnc', attn, Mv) + bv
        mean = out.mean(axis=(0, 1))
        var = out.var(axis=(0, 1))
        out = (out - mean) * jax.lax.rsqrt(var + EPS_BN) * gamma + beta
        out = out.reshape(b, h, w, c) + idn
        return jnp.where(out > 0, out, LEAK * out)

    def _gn(v, G=32, eps=1e-5):
        B_, H_, W_, C_ = v.shape
        g = v.reshape(B_, H_, W_, G, C_ // G)
        m = jnp.mean(g, axis=(1, 2, 4), keepdims=True)
        s = jnp.var(g, axis=(1, 2, 4), keepdims=True)
        return ((g - m) / jnp.sqrt(s + eps)).reshape(v.shape)

    def _ln_c(v, eps=1e-6):
        m = jnp.mean(v, axis=-1, keepdims=True)
        s = jnp.var(v, axis=-1, keepdims=True)
        return (v - m) / jnp.sqrt(s + eps)

    def _ln_t(v, eps=1e-5):
        m = jnp.mean(v, axis=-1, keepdims=True)
        s = jnp.var(v, axis=-1, keepdims=True)
        return (v - m) / jnp.sqrt(s + eps)

    def _to_tokens(v):
        B_, H_, W_, C_ = v.shape
        return v.reshape(B_, H_ * W_, C_)
    def _from_tokens(t, like):
        return t.reshape(like.shape)

    x = x + _L0_conv_ref(_gn(x), L0_conv_Wq, L0_conv_bq, L0_conv_Mk, L0_conv_Mv, L0_conv_bv, L0_conv_gamma, L0_conv_beta)
    return x


_drawn_inputs = setup_inputs


def setup_inputs(seed=0):
    import zlib

    import numpy as np

    out = dict(_drawn_inputs(seed))
    spreads = {'L0_conv_bq': (0.0, 0.1),
     'L0_conv_bv': (0.0, 0.1),
     'L0_conv_gamma': (1.0, 0.2),
     'L0_conv_beta': (0.0, 0.1)}
    factors = {}
    for name, (base, spread) in spreads.items():
        noise = np.random.default_rng([zlib.crc32(name.encode()), seed]).standard_normal(out[name].shape)
        drawn = base * np.exp(spread * noise) if base else spread * noise
        out[name] = jnp.asarray(drawn.astype(out[name].dtype))
    for name, factor in factors.items():
        out[name] = (out[name] * factor).astype(out[name].dtype)
    return out
```

```python
from contextlib import ExitStack

import concourse.bass as bass
from concourse import mybir

P = 128
F32 = mybir.dt.float32
F32R = mybir.dt.float32r
ALU = mybir.AluOpType
ACT = mybir.ActivationFunctionType
AX = mybir.AxisListType

EPS_GN = 1e-5
EPS_L1 = 1e-9
EPS_BN = 1e-5
LEAK = 0.2
GROUPS = 32

LAG_LOGITS = 10
LAG_EXP = 18
LAG_PROBS = 22
LAG_TURN = 23
LAG_SPLIT = 24
LAG_SPILL = 26
LAG_GRAM = 25
ATTN_SLOTS = 2
UNROLL1 = 16
UNROLL2 = 24
X2_SLOTS = 12
X2_AHEAD = 8
A2_SLOTS = 8
A2_AHEAD = 7


def gated_attention_kernel(nc, x, Wq, bq, Mk, Mv, bv, gamma, beta, out):
    B, H, W_, C = x.shape
    K = Mk.shape[0]
    CH = C // P
    TOK = H * W_
    ST = 4 * P
    SB = TOK // ST
    NS = B * SB
    NTOK = B * TOK
    GC = C // GROUPS
    assert CH == 4 and K == P and SB == 8 and NS % UNROLL1 == 0 and B % 3 == 1

    x_st = x.rearrange("b h w c -> (b h w) c").rearrange("(s p j) c -> s p (j c)", p=P, j=4)
    y_st = out.rearrange("b h w c -> (b h w) c").rearrange("(s p j) c -> s p (j c)", p=P, j=4)
    attn_dram = nc.dram_tensor("attn_spill", [NS, P, 4 * K], F32, kind="Internal").ap()

    with ExitStack() as ctx:
        def sb(name, shape, dt=F32):
            return ctx.enter_context(nc.sbuf_tensor(name, shape, dt))

        def sem(name):
            return ctx.enter_context(nc.semaphore(name))

        ring = sb("ring", [P, 16, CH * ST])
        stage = sb("stage", [P, 2, 4 * C])
        attn = sb("attn", [P, ATTN_SLOTS, 4 * K])
        attn_hl = sb("attn_hl", [P, 2, 4, 2, K], F32R)
        attn_acc = sb("attn_acc", [P, 4 * K])
        AT = sb("AT", [P, CH, K])
        ATs = sb("ATs", [P, 2, CH, K])
        MvT = sb("MvT", [P, C])
        MvC = sb("MvC", [P, CH, K])
        ident = sb("ident", [P, P])
        ones = sb("ones", [P, P])
        gavg = sb("gavg", [P, P])
        vecs = sb("vecs", [16, P])
        vcol = sb("vcol", [P, 4, CH])
        half_neg = sb("half_neg", [P, CH])
        bnst = sb("bnst", [P, 2, CH, SB, 6])
        chan = sb("chan", [P, CH, 2])
        dev = sb("dev", [P, CH])
        dev2 = sb("dev2", [P, CH])
        spread = sb("spread", [P, CH])
        var_e = sb("var_e", [P, CH])
        guess = sb("guess", [P, CH])
        nw1 = sb("nw1", [P, CH])
        nw2 = sb("nw2", [P, CH])
        nw3 = sb("nw3", [P, CH])
        rstd = sb("rstd", [P, B, CH])
        shift = sb("shift", [P, B, CH])
        rstd_cur = sb("rstd_cur", [P, 2, CH])
        shift_cur = sb("shift_cur", [P, 2, CH])
        bias0 = sb("bias0", [P, 1])
        lbias = sb("lbias", [P, 2])
        smax = sb("smax", [P, 2, SB])
        nmax = sb("nmax", [P, 2])
        esum = sb("esum", [P, 2, SB])
        esum1 = sb("esum1", [P, 2])
        einv = sb("einv", [P, 2])
        tsum = sb("tsum", [P, 4])
        tsum_e = sb("tsum_e", [P, 4])
        tinv = sb("tinv", [P, 4])
        mrow = sb("mrow", [1, K])
        mcol = sb("mcol", [P, 1])
        omean = sb("omean", [P, CH])
        bn_s = sb("bn_s", [P, CH])
        bn_d = sb("bn_d", [P, CH])
        bn_m = sb("bn_m", [P, CH])
        bn_t = sb("bn_t", [P, CH])
        gstd = sb("gstd", [P, B, CH])
        coef = sb("coef", [P, B, CH])
        Tcol = sb("Tcol", [P, B, CH])
        cur = sb("cur", [P, 3, 3, CH])

        with nc.sbuf_tensor("soft", [P, 16, ST], F32) as soft:
            pass
        attnT_hi = sb("attnT_hi", [P, 2, ST], F32R)
        attnT_lo = sb("attnT_lo", [P, 2, ST], F32R)
        Wout_hi = sb("Wout_hi", [P, 3, C], F32R)
        Wout_lo = sb("Wout_lo", [P, 3, C], F32R)
        MvS = sb("MvS", [P, CH, K])

        xs = stage[:, :, :].rearrange("p s (j c) -> p s j c", j=4)
        zs = stage[:, :, :].rearrange("p s (c n) -> p s c n", c=CH)
        attn2 = ring[:, X2_SLOTS:X2_SLOTS + 2, :].rearrange("p a (b n) -> p (a b) n", n=4 * K)
        prod = ring[:, 14, 0:C]
        gram, gram_hl, gram_hh, gram_half, cov = (ring[:, 14, C + i * K:C + (i + 1) * K] for i in range(5))
        WqS = ring[:, 12, :].rearrange("p (d c) -> p d c", d=CH)
        MkS = ring[:, 13, 0:C]
        MkT = ring[:, 13, 2 * C:3 * C].rearrange("p (d k) -> p d k", d=CH)

        ps = ctx.enter_context(nc.psum_tensor("ps", [P, 8, 512], F32))
        xtb = ps[:, 0:4, :]
        logit_b = ps[:, 4, :]
        turn_b = ps[:, 5, :]
        gram_b = ps[:, 6, 0:2 * K]
        misc = ps[:, 7, :]
        q_b = ps[:, 0:3, :]
        back_b = ps[:, 3:7, :]
        turn2_b = ps[:, 7, :]

        ident_zeroed = sem("ident_zeroed")
        consts_ready = sem("consts_ready")
        gavg_lower = sem("gavg_lower")
        mk_loaded, wq_loaded, mv_loaded, vecs_loaded = (sem(n) for n in ("mk_loaded", "wq_loaded", "mv_loaded", "vecs_loaded"))
        setup_psum = sem("setup_psum")
        setup_sbuf = sem("setup_sbuf")
        x_loaded = [sem(f"x_loaded{i}") for i in range(2)]
        xt_ready = sem("xt_ready")
        xt_copied = sem("xt_copied")
        stats_ready = sem("stats_ready")
        chan_ready = sem("chan_ready")
        gmean_ready = sem("gmean_ready")
        dev_ready = sem("dev_ready")
        dev2_ready = sem("dev2_ready")
        spread_ready = sem("spread_ready")
        gvar_ready = sem("gvar_ready")
        var_e_ready = sem("var_e_ready")
        guess_ready = sem("guess_ready")
        nw1_ready, nw2_ready, nw3_ready = (sem(f"nw{i}_ready") for i in (1, 2, 3))
        rstd_ready = sem("rstd_ready")
        shift_ready = sem("shift_ready")
        weights_ready = sem("weights_ready")
        cols_kept = sem("cols_kept")
        lshift_ready = sem("lshift_ready")
        lbias_ready = sem("lbias_ready")
        logits_ready = sem("logits_ready")
        logits_copied = sem("logits_copied")
        nmax_ready = sem("nmax_ready")
        exp_ready = sem("exp_ready")
        esum_ready = sem("esum_ready")
        einv_ready = sem("einv_ready")
        probs_ready = sem("probs_ready")
        turned = sem("turned")
        tsum_ready = sem("tsum_ready")
        tsum_e_ready = sem("tsum_e_ready")
        tinv_ready = sem("tinv_ready")
        attn_ready = sem("attn_ready")
        attn_hi_ready = sem("attn_hi_ready")
        attn_lo_ready = sem("attn_lo_ready")
        gram_done = sem("gram_done")
        acc_zeroed = sem("acc_zeroed")
        attn_added = sem("attn_added")
        attn_spilled = [sem(f"attn_spilled{i}") for i in range(ATTN_SLOTS)]
        gram_parts = sem("gram_parts")
        gram_turned = sem("gram_turned")
        bn_psum = sem("bn_psum")
        bn_sbuf = sem("bn_sbuf")
        bn_self = sem("bn_self")
        bn_guess = sem("bn_guess")
        x2_loaded = [sem(f"x2_loaded{i}") for i in range(X2_SLOTS)]
        y_stored = [sem(f"y_stored{i}") for i in range(X2_SLOTS)]
        attn2_loaded = [sem(f"attn2_loaded{i}") for i in range(A2_SLOTS)]
        attnT_ready = sem("attnT_ready")
        attnT_hi_ready = sem("attnT_hi_ready")
        attnT_lo_ready = sem("attnT_lo_ready")
        cur_ready = sem("cur_ready")
        MvS_ready = sem("MvS_ready")
        Wout_psum = sem("Wout_psum")
        Wout_hi_ready = sem("Wout_hi_ready")
        Wout_lo_ready = sem("Wout_lo_ready")
        q_filled = sem("q_filled")
        z_ready = sem("z_ready")
        leaky_done = sem("leaky_done")
        turned_back = sem("turned_back")
        y_ready = sem("y_ready")

        def in_range(k, j, lag, unroll=UNROLL1):
            return not isinstance(k, int) or 0 <= unroll * k + j - lag < NS

        def since(k, j, lag, unroll=UNROLL1):
            n = unroll * k + j - lag
            return None if isinstance(n, int) and n < 0 else n

        def pass1(eng, step):
            last = NS // UNROLL1
            for k in (0, 1):
                for j in range(UNROLL1):
                    step(k, j)
            with eng.Fori(2, last) as k:
                for j in range(UNROLL1):
                    step(k, j)
            for k in range(last, last + 2):
                for j in range(UNROLL1):
                    step(k, j)

        def pass2(eng, step):
            whole = NS // UNROLL2
            for j in range(UNROLL2):
                step(0, j)
            with eng.Fori(1, whole) as k:
                for j in range(UNROLL2):
                    step(k, j)
            for j in range(NS - whole * UNROLL2):
                step(whole, j)

        def batch(k, j, lag):
            return 2 * k + (j - lag) // SB

        block = ctx.enter_context(nc.Block())

        @block.sync
        def _(sp):
            sp.dma_start(stage[:, 0, :], x_st[0]).then_inc(x_loaded[0], 16)
            sp.dma_start(MkS, Mk).then_inc(mk_loaded, 16)
            for n, v in enumerate((bq, bv, gamma, beta)):
                sp.dma_start(vecs[CH * n:CH * n + CH, :], v.rearrange("(c p) -> c p", p=P)).then_inc(vecs_loaded, 16)
            sp.dma_start(MvC[:, :, :], Mv.rearrange("(c p) k -> p c k", p=P)).then_inc(mv_loaded, 16)
            sp.dma_start(stage[:, 1, :], x_st[1]).then_inc(x_loaded[1], 16)
            sp.dma_start(WqS, Wq.rearrange("(d p) c -> p d c", p=P)).then_inc(wq_loaded, 16)

            def load_x2(i):
                sp.wait_ge(logits_ready, NS - 16 + i + 1)
                sp.dma_start(ring[:, i, :], x_st[i]).then_inc(x2_loaded[i], 16)

            def step(k, j):
                s = since(k, j, 0)
                if in_range(k, j, 0) and not (isinstance(k, int) and s < 2):
                    sp.wait_ge(xt_ready, 2 * (s - 1))
                    sp.dma_start(stage[:, j % 2, :], x_st[s]).then_inc(x_loaded[j % 2], 16)
                if in_range(k, j, LAG_SPILL):
                    n, q = since(k, j, LAG_SPILL), (j - LAG_SPILL) % ATTN_SLOTS
                    sp.wait_ge(attn_ready, n + 1)
                    sp.dma_start(attn_dram[n], attn[:, q, :]).then_inc(attn_spilled[q], 16)
                if isinstance(k, int) and s >= NS:
                    at = s - (NS - 16) - LAG_LOGITS
                    for i in range(at + 1) if s == NS else [at]:
                        if i < X2_SLOTS:
                            load_x2(i)

            pass1(sp, step)
            for q in attn_spilled:
                sp.wait_ge(q, 16 * (NS // ATTN_SLOTS))
            sp.wait_ge(logits_ready, NS)
            for i in range(A2_AHEAD):
                sp.dma_start(attn2[:, i, :], attn_dram[i]).then_inc(attn2_loaded[i], 16)

            def step2(k, j):
                i = UNROLL2 * k + j
                static = isinstance(k, int)
                if not static or X2_SLOTS <= i + X2_AHEAD < NS:
                    n = X2_AHEAD + j
                    q = n % X2_SLOTS
                    sp.wait_ge(y_stored[q], 16 * (2 * k + n // X2_SLOTS))
                    sp.dma_start(ring[:, q, :], x_st[i + X2_AHEAD]).then_inc(x2_loaded[q], 16)
                if not static or i + A2_AHEAD < NS:
                    if not static or i >= 1:
                        sp.wait_ge(attnT_ready, i)
                    q = (j + A2_AHEAD) % A2_SLOTS
                    sp.dma_start(attn2[:, q, :], attn_dram[i + A2_AHEAD]).then_inc(attn2_loaded[q], 16)
                sp.wait_ge(y_ready, 2 * i + 2)
                sp.dma_start(y_st[i], ring[:, j % X2_SLOTS, :]).then_inc(y_stored[j % X2_SLOTS], 16)

            pass2(sp, step2)
            for q in range(X2_SLOTS):
                sp.wait_ge(y_stored[q], 16 * ((NS - q + X2_SLOTS - 1) // X2_SLOTS))

        @block.gpsimd
        def _(pool):
            pool.memset(ident[:, :], 0.0).then_inc(ident_zeroed, 1)
            pool.memset(gavg[:, :], 1.0 / GC).then_inc(ident_zeroed, 1)
            pool.memset(ones[:, :], 1.0).then_inc(consts_ready, 1)
            pool.memset(half_neg[:, :], -0.5).then_inc(consts_ready, 1)
            pool.wait_ge(ident_zeroed, 2)
            pool.affine_select(out=ident[:, :], in_=ident[:, :], compare_op=ALU.not_equal, fill=1.0, base=0,
                               pattern=[[-1, P]], channel_multiplier=1).then_inc(consts_ready, 1)
            gv = gavg[:, :].rearrange("p (g c) -> p g c", c=GC)
            pool.affine_select(out=gv, in_=gv, compare_op=ALU.is_ge, fill=0.0, base=0,
                               pattern=[[-GC, P // GC], [0, GC]], channel_multiplier=1).then_inc(gavg_lower, 1)
            pool.wait_ge(gavg_lower, 1)
            pool.affine_select(out=gv, in_=gv, compare_op=ALU.is_ge, fill=0.0, base=GC - 1,
                               pattern=[[GC, P // GC], [0, GC]], channel_multiplier=-1).then_inc(consts_ready, 1)
            pool.memset(attn_acc[:, :], 0.0).then_inc(acc_zeroed, 1)
            pool.wait_ge(acc_zeroed, 1)

            def step(k, j):
                if j % SB == 1 and in_range(k, j, SB + 1):
                    pool.wait_ge(var_e_ready, batch(k, j, SB + 1) + 1)
                    pool.tensor_tensor(guess[:, :], var_e[:, :], half_neg[:, :], ALU.pow).then_inc(guess_ready, 1)
                if j % SB == LAG_PROBS % SB and in_range(k, j, LAG_PROBS):
                    pool.wait_ge(einv_ready, batch(k, j, LAG_PROBS) + 1)
                if in_range(k, j, LAG_SPLIT):
                    n, q = since(k, j, LAG_SPLIT), (j - LAG_SPLIT) % ATTN_SLOTS
                    pool.wait_ge(attn_ready, n + 1)
                    if not isinstance(k, int) or n >= 1:
                        pool.wait_ge(attn_added, n)
                    pool.tensor_tensor(attn_acc[:, :], attn_acc[:, :], attn[:, q, :], ALU.add).then_inc(attn_added, 1)
                    pool.wait_ge(attn_hi_ready, n + 1)
                    pool.tensor_tensor(attn_hl[:, q % 2, :, 1, :], attn[:, q, :].rearrange("p (t k) -> p t k", t=4),
                                       attn_hl[:, q % 2, :, 0, :], ALU.subtract).then_inc(attn_lo_ready, 1)
                if in_range(k, j, LAG_PROBS):
                    q = (j - LAG_PROBS) % 16
                    b2 = ((j - LAG_PROBS) // SB) % 2
                    pool.tensor_scalar(soft[:, q, :], soft[:, q, :], einv[:, b2:b2 + 1], 1.0, ALU.mult,
                                       ALU.mult).then_inc(probs_ready, 1)

            pass1(pool, step)
            pool.wait_ge(bn_sbuf, 5)
            pool.tensor_tensor(guess[:, :], var_e[:, :], half_neg[:, :], ALU.pow).then_inc(bn_guess, 1)

        @block.tensor
        def _(pe):
            pe.wait_ge(consts_ready, 4)

            def setup():
                pe.wait_ge(mk_loaded, 16)
                for d in range(CH):
                    mm = pe.transpose(misc[:, d * P:(d + 1) * P], MkS[:, d * P:(d + 1) * P], ident[:, :])
                mm.then_inc(setup_psum, 1)
                pe.wait_ge(mv_loaded, 16)
                for c in range(CH):
                    mm = pe.transpose(logit_b[:, c * P:(c + 1) * P], MvC[:, c, :], ident[:, :])
                mm.then_inc(setup_psum, 1)
                pe.wait_ge(vecs_loaded, 64)
                pe.transpose(turn_b[:, 0:16], vecs[:, :], ident[0:16, 0:16]).then_inc(setup_psum, 1)
                pe.wait_ge(wq_loaded, 16)
                pe.wait_ge(setup_sbuf, 3)
                for c in range(CH):
                    for d in range(CH):
                        mm = pe.matmul(misc[:, c * K:(c + 1) * K], WqS[:, d, c * P:(c + 1) * P], MkT[:, d, :],
                                       start=(d == 0), stop=(d == CH - 1))
                mm.then_inc(setup_psum, 1)
                for d in range(CH):
                    mm = pe.matmul(turn_b[:, 16:17], MkT[:, d, :], vcol[:, 0, d:d + 1], start=(d == 0), stop=(d == CH - 1))
                mm.then_inc(setup_psum, 1)
                pe.wait_ge(setup_sbuf, 5)

            def step(k, j):
                if isinstance(k, int) and UNROLL1 * k + j == 3:
                    setup()
                s = since(k, j, 0)
                if in_range(k, j, 0):
                    pe.wait_ge(x_loaded[j % 2], 16 * (8 * k + j // 2 + 1))
                    for h in range(2):
                        if not isinstance(k, int) or s >= 1:
                            pe.wait_ge(xt_copied, 2 * s + h - 1)
                        for c in (2 * h, 2 * h + 1):
                            for t in range(4):
                                mm = pe.transpose(xtb[:, c, t * P:(t + 1) * P], xs[:, j % 2, t, c * P:(c + 1) * P],
                                                  ident[:, :])
                        mm.then_inc(xt_ready, 1)
                if j % SB == 2 and in_range(k, j, SB + 2):
                    pe.wait_ge(shift_ready, batch(k, j, SB + 2) + 1)
                    par = ((j - SB - 2) // SB) % 2
                    for c in range(CH):
                        mm = pe.matmul(misc[:, 16:17], AT[:, c, :], shift_cur[:, par, c:c + 1], start=(c == 0), stop=(c == CH - 1))
                    mm.then_inc(lshift_ready, 1)
                if in_range(k, j, LAG_LOGITS):
                    n, q = since(k, j, LAG_LOGITS), (j - LAG_LOGITS) % 16
                    par = ((j - LAG_LOGITS) // SB) % 2
                    if (j - LAG_LOGITS) % SB == 0:
                        pe.wait_ge(weights_ready, batch(k, j, LAG_LOGITS) + 1)
                    if not isinstance(k, int) or n >= 1:
                        pe.wait_ge(logits_copied, n)
                    for c in range(CH):
                        mm = pe.matmul(logit_b, ATs[:, par, c, :], ring[:, q, c * ST:(c + 1) * ST],
                                       start=(c == 0), stop=(c == CH - 1))
                    mm.then_inc(logits_ready, 1)
                if j % SB == 0 and in_range(k, j, SB):
                    pe.wait_ge(chan_ready, batch(k, j, SB) + 1)
                    pe.matmul(misc[:, 0:CH], gavg[:, :], chan[:, :, 0], start=True, stop=True).then_inc(gmean_ready, 1)
                if in_range(k, j, LAG_GRAM):
                    n, q = since(k, j, LAG_GRAM), (j - LAG_GRAM) % 2
                    pe.wait_ge(attn_lo_ready, n + 1)
                    for t in range(4):
                        mm = pe.matmul(gram_b, attn_hl[:, q, t, 0, :], attn_hl[:, q, t, :, :],
                                       start=(isinstance(k, int) and n == 0 and t == 0),
                                       stop=(isinstance(k, int) and n == NS - 1 and t == 3), skip_group_check=True)
                    mm.then_inc(gram_done, 1)
                if in_range(k, j, LAG_TURN):
                    n, q = since(k, j, LAG_TURN), (j - LAG_TURN) % 16
                    pe.wait_ge(probs_ready, n + 1)
                    if not isinstance(k, int) or n >= 1:
                        pe.wait_ge(attn_ready, n)
                    for t in range(4):
                        mm = pe.transpose(turn_b[:, t * P:(t + 1) * P], soft[:, q, t * P:(t + 1) * P], ident[:, :])
                    mm.then_inc(turned, 1)
                if j % SB == 0 and in_range(k, j, SB):
                    pe.wait_ge(spread_ready, batch(k, j, SB) + 1)
                    pe.matmul(misc[:, 8:8 + CH], gavg[:, :], spread[:, :], start=True, stop=True).then_inc(gvar_ready, 1)

            pass1(pe, step)

            pe.wait_ge(attn_added, NS)
            for t in range(4):
                pe.matmul(misc[0:1, 0:K], ones[:, 0:1], attn_acc[:, t * K:(t + 1) * K], start=(t == 0), stop=(t == 3))
            for t in range(4):
                mm = pe.matmul(misc[:, K:K + 1], attn_acc[:, t * K:(t + 1) * K], ones[:, 0:1], start=(t == 0), stop=(t == 3))
            mm.then_inc(bn_psum, 1)
            pe.wait_ge(gram_parts, 1)
            pe.transpose(turn_b[:, 0:K], gram_hl, ident[:, :]).then_inc(gram_turned, 1)
            pe.wait_ge(bn_sbuf, 2)
            pe.matmul(misc[:, 2 * K:3 * K], mrow[:, :], mrow[:, :], start=True, stop=True).then_inc(bn_psum, 1)
            pe.wait_ge(bn_sbuf, 3)
            pe.matmul(turn_b, cov, MvT[:, :], start=True, stop=True).then_inc(bn_psum, 1)
            pe.wait_ge(bn_sbuf, 4)
            for c in range(CH):
                pe.matmul(misc[:, 3 * K + c:3 * K + c + 1], prod[:, c * P:(c + 1) * P], ones[:, 0:1], start=True, stop=True)
            for c in range(CH):
                mm = pe.matmul(misc[:, 3 * K + 8 + c:3 * K + 9 + c], MvT[:, c * P:(c + 1) * P], mcol[:, :], start=True, stop=True)
            mm.then_inc(bn_psum, 1)

            def weights(b):
                pe.wait_ge(MvS_ready, b + 1)
                for c in range(CH):
                    mm = pe.transpose(turn2_b[:, c * P:(c + 1) * P], MvS[:, c, :], ident[:, :])
                mm.then_inc(Wout_psum, 1)

            def turn_attn(k, j):
                i = UNROLL2 * k + j
                pe.wait_ge(attn2_loaded[j % A2_SLOTS], 16 * (3 * k + j // A2_SLOTS + 1))
                if j % SB == 5 and (not isinstance(k, int) or i - 2 + SB < NS):
                    pe.wait_ge(Wout_lo_ready, 3 * k + j // SB + 2)
                elif not isinstance(i, int) or i >= 1:
                    pe.wait_ge(attnT_lo_ready, i)
                for t in range(4):
                    mm = pe.transpose(turn2_b[:, t * P:(t + 1) * P], attn2[:, j % A2_SLOTS, t * K:(t + 1) * K], ident[:, :])
                mm.then_inc(attnT_ready, 1)

            weights(0)
            pe.wait_ge(Wout_lo_ready, 1)
            turn_attn(0, 0)

            def turn_back(k, j, h):
                i = UNROLL2 * k + j
                if h == 0:
                    pe.wait_ge(leaky_done, 2 * i + 2)
                if not isinstance(i, int) or i >= 1:
                    pe.wait_ge(y_ready, 2 * i - 1 + h)
                for t in (2 * h, 2 * h + 1):
                    for c in range(CH):
                        mm = pe.transpose(back_b[:, t, c * P:(c + 1) * P], zs[:, j % 2, c, t * P:(t + 1) * P], ident[:, :])
                mm.then_inc(turned_back, 1)

            def step2(k, j):
                i = UNROLL2 * k + j
                static = isinstance(k, int)
                if not static or i + 1 < NS:
                    turn_attn(k, j + 1)
                pe.wait_ge(x2_loaded[j % X2_SLOTS], 16 * (2 * k + j // X2_SLOTS + 1))
                if j % SB == 0:
                    pe.wait_ge(Wout_lo_ready, 3 * k + j // SB + 1)
                for c in range(CH):
                    m = 4 * j + c
                    if not static or 4 * i + c >= 3:
                        pe.wait_ge(z_ready, 4 * i + c - 2)
                    for t in range(4):
                        xt = ring[:, j % X2_SLOTS, t * C + c * P:t * C + (c + 1) * P]
                        pe.matmul(q_b[:, m % 3, t * P:(t + 1) * P], xt, ident[:, :], is_transpose=True,
                                  start=(t == 0), stop=False, skip_group_check=True)
                    if c == 0:
                        pe.wait_ge(attnT_lo_ready, i + 1)
                    W_hi, W_lo = (W[:, j // SB, c * P:(c + 1) * P] for W in (Wout_hi, Wout_lo))
                    pe.matmul(q_b[:, m % 3, :], W_hi, attnT_hi[:, j % 2, :], start=False, stop=False, skip_group_check=True)
                    pe.matmul(q_b[:, m % 3, :], W_hi, attnT_lo[:, j % 2, :], start=False, stop=False, skip_group_check=True)
                    pe.matmul(q_b[:, m % 3, :], W_lo, attnT_hi[:, j % 2, :], start=False, stop=True, skip_group_check=True)\
                      .then_inc(q_filled, 1)
                    if c % 2 and (not static or i >= 1):
                        turn_back(k, j - 1, c // 2)
                    if c == 1 and j % SB == 3 and (not static or i + SB < NS):
                        pe.wait_ge(attnT_lo_ready, i + 2)
                        weights(3 * k + j // SB + 1)

            pass2(pe, step2)
            last = NS - 1
            for h in range(2):
                turn_back(last // UNROLL2, last % UNROLL2, h)

        @block.scalar
        def _(act):
            def step(k, j):
                s = since(k, j, 0)
                if in_range(k, j, 0):
                    if not isinstance(k, int) or s >= 16:
                        act.wait_ge(logits_ready, s - 15)
                    for h in range(2):
                        act.wait_ge(xt_ready, 2 * s + h + 1)
                        act.activation(ring[:, j, 2 * h * ST:2 * (h + 1) * ST].rearrange("p (c n) -> p c n", c=2),
                                       xtb[:, 2 * h:2 * h + 2, :], ACT.Copy).then_inc(xt_copied, 1)
                if in_range(k, j, LAG_SPLIT):
                    n, q = since(k, j, LAG_SPLIT), (j - LAG_SPLIT) % ATTN_SLOTS
                    act.wait_ge(attn_ready, n + 1)
                    if not isinstance(k, int) or n >= 2:
                        act.wait_ge(gram_done, n - 1)
                    act.activation(attn_hl[:, q % 2, :, 0, :], attn[:, q, :].rearrange("p (t k) -> p t k", t=4),
                                   ACT.Copy).then_inc(attn_hi_ready, 1)
                g = (j - LAG_EXP) % SB
                if g < SB // 2 and in_range(k, j, LAG_EXP):
                    b, par = batch(k, j, LAG_EXP), ((j - LAG_EXP) // SB) % 2
                    if g == 0:
                        act.wait_ge(nmax_ready, b + 1)
                    for e in (2 * g, 2 * g + 1):
                        q = SB * par + e
                        act.activation(soft[:, q, :], soft[:, q, :], ACT.Exp, bias=nmax[:, par:par + 1],
                                       accum_out=esum[:, par, e:e + 1]).then_inc(exp_ready, 1)

            pass1(act, step)

            def copy_weights(b, b3):
                act.wait_ge(Wout_psum, b + 1)
                act.activation(Wout_hi[:, b3, :], turn2_b, ACT.Copy).then_inc(Wout_hi_ready, 1)

            def copy_attnT(k, j):
                i = UNROLL2 * k + j
                act.wait_ge(attnT_ready, i + 1)
                if not isinstance(i, int) or i >= 2:
                    act.wait_ge(q_filled, 4 * i - 4)
                act.activation(attnT_hi[:, j % 2, :], turn2_b, ACT.Copy).then_inc(attnT_hi_ready, 1)

            copy_weights(0, 0)
            copy_attnT(0, 0)

            def step2(k, j):
                i = UNROLL2 * k + j
                static = isinstance(k, int)
                if not static or i + 1 < NS:
                    copy_attnT(k, j + 1)
                b3 = j // SB
                for c in range(CH):
                    act.wait_ge(q_filled, 4 * i + c + 1)
                    if c == 0 and (not static or i >= 2):
                        act.wait_ge(turned_back, 2 * i - 2)
                    act.activation(zs[:, j % 2, c, :], q_b[:, (4 * j + c) % 3, :], ACT.Identity,
                                   bias=cur[:, b3, 1, c:c + 1], scale=cur[:, b3, 0, c:c + 1]).then_inc(z_ready, 1)
                    if c == 1 and j % SB == 3 and (not static or i + SB < NS):
                        copy_weights(3 * k + b3 + 1, (b3 + 1) % 3)

            pass2(act, step2)

        @block.vector
        def _(dve):
            dve.wait_ge(consts_ready, 4)

            def setup():
                dve.wait_ge(setup_psum, 1)
                dve.tensor_copy(ring[:, 13, 2 * C:3 * C], misc).then_inc(setup_sbuf, 1)
                dve.wait_ge(setup_psum, 2)
                dve.tensor_copy(MvT[:, :], logit_b).then_inc(setup_sbuf, 1)
                dve.wait_ge(setup_psum, 3)
                dve.tensor_copy(vcol[:, :, :].rearrange("p v c -> p (v c)"), turn_b[:, 0:16]).then_inc(setup_sbuf, 1)
                dve.wait_ge(setup_psum, 4)
                dve.tensor_copy(AT[:, :, :].rearrange("p c k -> p (c k)"), misc).then_inc(setup_sbuf, 1)
                dve.wait_ge(setup_psum, 5)
                dve.tensor_copy(bias0[:, :], turn_b[:, 16:17]).then_inc(setup_sbuf, 1)
                dve.wait_ge(setup_sbuf, 5)

            def newton(n, done):
                dve.tensor_tensor(nw1[:, :], guess[:, :], guess[:, :], ALU.mult).then_inc(nw1_ready, 1)
                dve.wait_ge(nw1_ready, n)
                dve.tensor_tensor(nw2[:, :], nw1[:, :], var_e[:, :], ALU.mult).then_inc(nw2_ready, 1)
                dve.wait_ge(nw2_ready, n)
                dve.tensor_scalar(nw3[:, :], nw2[:, :], -0.5, 1.5, ALU.mult, ALU.add).then_inc(nw3_ready, 1)
                dve.wait_ge(nw3_ready, n)
                dve.tensor_tensor(done, guess[:, :], nw3[:, :], ALU.mult).then_inc(rstd_ready, 1)
                dve.wait_ge(rstd_ready, n)

            def step(k, j):
                static = isinstance(k, int)
                if static and UNROLL1 * k + j == 3:
                    setup()
                s = since(k, j, 0)
                complete = j % SB == 0 and in_range(k, j, SB)
                if complete:
                    dve.wait_ge(stats_ready, s)

                def aggregate():
                    par = ((j - SB) // SB) % 2
                    for c in range(CH):
                        ins = dve.bn_aggr(chan[:, c, :], bnst[:, par, c, :, :].rearrange("p g f -> p (g f)"))
                    ins.then_inc(chan_ready, 1)

                if in_range(k, j, 0):
                    for h in range(2):
                        dve.wait_ge(xt_copied, 2 * s + h + 1)
                        for c in (2 * h, 2 * h + 1):
                            ins = dve.bn_stats(bnst[:, j // SB, c, j % SB, :], ring[:, j, c * ST:(c + 1) * ST])
                            if complete and c == 0:
                                aggregate()
                    ins.then_inc(stats_ready, 1)
                elif complete:
                    aggregate()
                if j % SB == 1 and in_range(k, j, SB + 1):
                    b, par = batch(k, j, SB + 1), ((j - SB - 1) // SB) % 2
                    dve.wait_ge(gvar_ready, b + 1)
                    dve.tensor_scalar(var_e[:, :], misc[:, 8:8 + CH], EPS_GN, None, ALU.add).then_inc(var_e_ready, 1)
                    dve.wait_ge(var_e_ready, b + 1)
                    dve.wait_ge(guess_ready, b + 1)
                    newton(b + 1, rstd_cur[:, par, :])
                    dve.tensor_tensor(shift_cur[:, par, :], misc[:, 0:CH], rstd_cur[:, par, :], ALU.mult)\
                       .then_inc(shift_ready, 1)
                    dve.tensor_tensor(ATs[:, par, :, :], AT[:, :, :],
                                      rstd_cur[:, par, :].unsqueeze(2).to_broadcast([P, CH, K]),
                                      ALU.mult).then_inc(weights_ready, 1)
                    dve.wait_ge(shift_ready, b + 1)
                    dve.tensor_copy(rstd[:, bass.ds(b, 1), :], rstd_cur[:, par:par + 1, :])
                    dve.tensor_tensor(gstd[:, bass.ds(b, 1), :], var_e[:, :].unsqueeze(1), rstd_cur[:, par:par + 1, :],
                                      ALU.mult)
                    dve.tensor_copy(shift[:, bass.ds(b, 1), :], shift_cur[:, par:par + 1, :]).then_inc(cols_kept, 1)
                if j % SB == 2 and in_range(k, j, SB + 2):
                    b1, par1 = batch(k, j, SB + 2), ((j - SB - 2) // SB) % 2
                    dve.wait_ge(lshift_ready, b1 + 1)
                    dve.tensor_tensor(lbias[:, par1:par1 + 1], bias0[:, :], misc[:, 16:17], ALU.subtract)\
                       .then_inc(lbias_ready, 1)
                if in_range(k, j, LAG_LOGITS):
                    n, q = since(k, j, LAG_LOGITS), (j - LAG_LOGITS) % 16
                    g, parl = (j - LAG_LOGITS) % SB, ((j - LAG_LOGITS) // SB) % 2
                    bl = batch(k, j, LAG_LOGITS)
                    dve.wait_ge(lbias_ready, bl + 1)
                    dve.wait_ge(logits_ready, n + 1)
                    if not static or n >= 16:
                        dve.wait_ge(turned, n - 15)
                    dve.tensor_scalar(soft[:, q, :], logit_b, lbias[:, parl:parl + 1], None, ALU.add, ALU.max,
                                      accum_out=smax[:, parl, g:g + 1]).then_inc(logits_copied, 1)
                    if g == SB - 1:
                        dve.wait_ge(logits_copied, n + 1)
                        dve.tensor_reduce(nmax[:, parl:parl + 1], smax[:, parl, :], AX.X, ALU.max, negate=True)\
                           .then_inc(nmax_ready, 1)
                if complete:
                    b = batch(k, j, SB)
                    dve.wait_ge(gmean_ready, b + 1)
                    dve.tensor_tensor(dev[:, :], chan[:, :, 0], misc[:, 0:CH], ALU.subtract).then_inc(dev_ready, 1)
                    dve.wait_ge(dev_ready, b + 1)
                    dve.tensor_tensor(dev2[:, :], dev[:, :], dev[:, :], ALU.mult).then_inc(dev2_ready, 1)
                    dve.wait_ge(dev2_ready, b + 1)
                    dve.tensor_tensor(spread[:, :], dev2[:, :], chan[:, :, 1], ALU.add).then_inc(spread_ready, 1)
                if in_range(k, j, LAG_TURN):
                    n, q = since(k, j, LAG_TURN), (j - LAG_TURN) % ATTN_SLOTS
                    tb = turn_b.rearrange("p (t k) -> p t k", t=4)
                    dve.wait_ge(turned, n + 1)
                    dve.tensor_reduce(tsum[:, :], tb, AX.X, ALU.add).then_inc(tsum_ready, 1)
                    dve.wait_ge(tsum_ready, n + 1)
                    dve.tensor_scalar(tsum_e[:, :], tsum[:, :], EPS_L1, None, ALU.add).then_inc(tsum_e_ready, 1)
                    dve.wait_ge(tsum_e_ready, n + 1)
                    dve.reciprocal(tinv[:, :], tsum_e[:, :]).then_inc(tinv_ready, 1)
                    dve.wait_ge(tinv_ready, n + 1)
                    if not static or n >= ATTN_SLOTS:
                        dve.wait_ge(attn_spilled[q], 16 * (UNROLL1 // ATTN_SLOTS * k + (j - LAG_TURN) // ATTN_SLOTS))
                        dve.wait_ge(attn_lo_ready, n - ATTN_SLOTS + 1)
                    dve.tensor_tensor(attn[:, q, :].rearrange("p (t k) -> p t k", t=4), tb,
                                      tinv[:, :].unsqueeze(2).to_broadcast([P, 4, K]), ALU.mult).then_inc(attn_ready, 1)
                if (j - LAG_PROBS) % SB == 0 and in_range(k, j, LAG_PROBS):
                    bp, parp = batch(k, j, LAG_PROBS), ((j - LAG_PROBS) // SB) % 2
                    dve.wait_ge(exp_ready, SB * (bp + 1))
                    dve.tensor_reduce(esum1[:, parp:parp + 1], esum[:, parp, :], AX.X, ALU.add).then_inc(esum_ready, 1)
                    dve.wait_ge(esum_ready, bp + 1)
                    dve.reciprocal(einv[:, parp:parp + 1], esum1[:, parp:parp + 1]).then_inc(einv_ready, 1)

            pass1(dve, step)

            dve.wait_ge(gram_done, NS)
            dve.tensor_scalar(gram_hl, gram_b[:, K:2 * K], 1.0 / NTOK, None, ALU.mult).then_inc(gram_parts, 1)
            dve.tensor_scalar(gram_hh, gram_b[:, 0:K], 1.0 / NTOK, None, ALU.mult).then_inc(gram_parts, 1)
            dve.wait_ge(gram_parts, 2)
            dve.tensor_tensor(gram_half, gram_hh, gram_hl, ALU.add).then_inc(gram_parts, 1)
            dve.wait_ge(gram_parts, 3)
            dve.wait_ge(gram_turned, 1)
            dve.tensor_tensor(gram, gram_half, turn_b[:, 0:K], ALU.add).then_inc(gram_parts, 1)
            dve.wait_ge(gram_parts, 4)
            dve.wait_ge(bn_psum, 1)
            dve.tensor_scalar(mrow[:, :], misc[0:1, 0:K], 1.0 / NTOK, None, ALU.mult).then_inc(bn_sbuf, 1)
            dve.tensor_scalar(mcol[:, :], misc[:, K:K + 1], 1.0 / NTOK, None, ALU.mult).then_inc(bn_sbuf, 1)
            dve.wait_ge(bn_sbuf, 2)
            dve.wait_ge(bn_psum, 2)
            dve.tensor_tensor(cov, gram, misc[:, 2 * K:3 * K], ALU.subtract).then_inc(bn_sbuf, 1)
            dve.wait_ge(bn_psum, 3)
            dve.tensor_tensor(prod, turn_b, MvT[:, :], ALU.mult).then_inc(bn_sbuf, 1)
            dve.wait_ge(bn_psum, 4)
            dve.tensor_scalar(var_e[:, :], misc[:, 3 * K:3 * K + CH], EPS_BN, None, ALU.add).then_inc(bn_sbuf, 1)
            dve.tensor_tensor(omean[:, :], misc[:, 3 * K + 8:3 * K + 8 + CH], vcol[:, 1, :], ALU.add).then_inc(bn_self, 1)
            dve.wait_ge(bn_sbuf, 5)
            dve.wait_ge(bn_guess, 1)
            newton(B + 1, bn_m[:, :])
            dve.tensor_tensor(bn_s[:, :], bn_m[:, :], vcol[:, 2, :], ALU.mult).then_inc(bn_sbuf, 1)
            dve.wait_ge(bn_sbuf, 6)
            dve.wait_ge(bn_self, 1)
            dve.tensor_tensor(bn_d[:, :], vcol[:, 1, :], omean[:, :], ALU.subtract).then_inc(bn_self, 1)
            dve.wait_ge(bn_self, 2)
            dve.tensor_tensor(dev[:, :], bn_d[:, :], bn_s[:, :], ALU.mult).then_inc(bn_self, 1)
            dve.wait_ge(bn_self, 3)
            dve.tensor_tensor(bn_t[:, :], dev[:, :], vcol[:, 3, :], ALU.add).then_inc(bn_self, 1)
            dve.wait_ge(bn_self, 4)
            dve.wait_ge(cols_kept, B)
            dve.tensor_tensor(Tcol[:, :, :], bn_t[:, :].unsqueeze(1).to_broadcast([P, B, CH]), shift[:, :, :],
                              ALU.subtract).then_inc(bn_self, 1)
            dve.tensor_tensor(coef[:, :, :], bn_s[:, :].unsqueeze(1).to_broadcast([P, B, CH]), gstd[:, :, :],
                              ALU.mult).then_inc(bn_self, 1)
            dve.wait_ge(bn_self, 6)

            def columns(b, b3):
                dve.tensor_copy(cur[:, b3, 0:1, :], rstd[:, bass.ds(b, 1), :])
                dve.tensor_copy(cur[:, b3, 1:2, :], Tcol[:, bass.ds(b, 1), :])
                dve.tensor_copy(cur[:, b3, 2:3, :], coef[:, bass.ds(b, 1), :]).then_inc(cur_ready, 1)
                dve.wait_ge(cur_ready, b + 1)
                if not isinstance(b, int) or b >= 1:
                    dve.wait_ge(Wout_psum, b)
                dve.tensor_tensor(MvS[:, :, :], MvC[:, :, :], cur[:, b3, 2, :].unsqueeze(2).to_broadcast([P, CH, K]),
                                  ALU.mult).then_inc(MvS_ready, 1)

            def split_weights(b, b3):
                dve.wait_ge(Wout_hi_ready, b + 1)
                dve.tensor_tensor(Wout_lo[:, b3, :], turn2_b, Wout_hi[:, b3, :], ALU.subtract).then_inc(Wout_lo_ready, 1)

            def split_attn(k, j):
                dve.wait_ge(attnT_hi_ready, UNROLL2 * k + j + 1)
                dve.tensor_tensor(attnT_lo[:, j % 2, :], turn2_b, attnT_hi[:, j % 2, :], ALU.subtract)\
                   .then_inc(attnT_lo_ready, 1)

            columns(0, 0)
            split_weights(0, 0)
            split_attn(0, 0)

            def finish(k, j, h):
                xh = ring[:, j % X2_SLOTS, 2 * h * C:2 * (h + 1) * C].rearrange("p (t c) -> p t c", t=2)
                dve.wait_ge(turned_back, 2 * (UNROLL2 * k + j) + h + 1)
                dve.tensor_tensor(xh, back_b[:, 2 * h:2 * h + 2, :], xh, ALU.add).then_inc(y_ready, 1)

            def step2(k, j):
                i = UNROLL2 * k + j
                static = isinstance(k, int)
                if not static or i + 1 < NS:
                    split_attn(k, j + 1)
                for h in range(2):
                    z = zs[:, j % 2, 2 * h:2 * h + 2, :]
                    dve.wait_ge(z_ready, 4 * i + 2 * h + 2)
                    dve.scalar_tensor_tensor(out=z, in0=z, scalar=LEAK, in1=z, op0=ALU.mult, op1=ALU.max)\
                       .then_inc(leaky_done, 1)
                    if not static or i >= 1:
                        finish(k, j - 1, h)
                    if h == 0 and j % SB == 3 and (not static or i + SB < NS):
                        split_weights(3 * k + j // SB + 1, (j // SB + 1) % 3)
                if j % SB == 2 and (not static or i + SB < NS):
                    columns(3 * k + j // SB + 1, (j // SB + 1) % 3)

            pass2(dve, step2)
            last = NS - 1
            for h in range(2):
                finish(last // UNROLL2, last % UNROLL2, h)


_INS = ["x", "L0_conv_Wq", "L0_conv_bq", "L0_conv_Mk", "L0_conv_Mv", "L0_conv_bv", "L0_conv_gamma", "L0_conv_beta"]


def kernel(**inputs):
    import numpy as _np
    import concourse.bacc as _bacc
    from concourse import mybir as _mybir
    from concourse.bass_utils import run_bass_kernel_spmd as _run

    nc = _bacc.Bacc("TRN2", target_bir_lowering=False, num_devices=1)
    arrays, args = {}, []
    for name in _INS:
        a = _np.ascontiguousarray(inputs[name])
        arrays[f"in_{name}_dram"] = a
        args.append(nc.dram_tensor(f"in_{name}_dram", a.shape, _mybir.dt.from_np(a.dtype), kind="ExternalInput").ap())
    shape = inputs["x"].shape
    args.append(nc.dram_tensor("out_0_dram", shape, _mybir.dt.float32, kind="ExternalOutput").ap())
    gated_attention_kernel(nc, *args)
    r = _run(nc, [arrays], core_ids=[0])
    return r.results[0]["out_0_dram"]
```

```python
from contextlib import ExitStack

import concourse.bass as bass
from concourse import mybir

P = 128
F32 = mybir.dt.float32
F32R = mybir.dt.float32r
ALU = mybir.AluOpType
ACT = mybir.ActivationFunctionType
AX = mybir.AxisListType

EPS_GN = 1e-5
EPS_L1 = 1e-9
EPS_BN = 1e-5
LEAK = 0.2
GROUPS = 32

LAG_XSPLIT = 8
LAG_LOGITS = 10
LAG_EXP = 18
LAG_PROBS = 20
LAG_TURN = 21
LAG_SPLIT = 22
LAG_GRAM = 23
LAG_SPILL = 24
LAG_LOAD = -1
XSPLIT = 2
STAGE = 3
SOFT = 12
ATTN_SLOTS = 3
ROT = 3
DRAIN = 16
UNROLL1 = 24
UNROLL2 = 24
X_SLOTS = 12
X2_AHEAD = 8
A2_SLOTS = 8
A2_AHEAD = 7


def gated_attention_kernel(nc, x, Wq, bq, Mk, Mv, bv, gamma, beta, out):
    B, H, W_, C = x.shape
    K = Mk.shape[0]
    CH = C // P
    TOK = H * W_
    ST = 4 * P
    SB = TOK // ST
    NS = B * SB
    NTOK = B * TOK
    GC = C // GROUPS
    assert CH == 4 and K == P and SB == 8 and ROT * SB == UNROLL1 == UNROLL2 and B % 3 == 1

    x_st = x.rearrange("b h w c -> (b h w) c").rearrange("(s p j) c -> s p (j c)", p=P, j=4)
    y_st = out.rearrange("b h w c -> (b h w) c").rearrange("(s p j) c -> s p (j c)", p=P, j=4)
    attn_dram = nc.dram_tensor("attn_spill", [NS, P, 4 * K], F32, kind="Internal").ap()

    with ExitStack() as ctx:
        def sb(name, shape, dt=F32):
            return ctx.enter_context(nc.sbuf_tensor(name, shape, dt))

        def sem(name):
            return ctx.enter_context(nc.semaphore(name))

        ring = sb("ring", [P, X_SLOTS, CH * ST])
        stage = sb("stage", [P, STAGE, 4 * C])
        attn = sb("attn", [P, ATTN_SLOTS, 4 * K])
        attn_hl = sb("attn_hl", [P, 2, 4, 2, K], F32R)
        attn_acc = sb("attn_acc", [P, 4 * K])
        AT = sb("AT", [P, CH, K])
        ATs = sb("ATs", [P, ROT, CH, K])
        MvT = sb("MvT", [P, C])
        ident = sb("ident", [P, P])
        ones = sb("ones", [P, P])
        gavg = sb("gavg", [P, P])
        vecs = sb("vecs", [16, P])
        vcol = sb("vcol", [P, 4, CH])
        half_neg = sb("half_neg", [P, CH])
        bnst = sb("bnst", [P, ROT, CH, SB, 6])
        chan = sb("chan", [P, CH, 2])
        dev = sb("dev", [P, CH])
        dev2 = sb("dev2", [P, CH])
        spread = sb("spread", [P, CH])
        var_e = sb("var_e", [P, CH])
        guess = sb("guess", [P, CH])
        nw1 = sb("nw1", [P, CH])
        nw2 = sb("nw2", [P, CH])
        nw3 = sb("nw3", [P, CH])
        rstd = sb("rstd", [P, B, CH])
        shift = sb("shift", [P, B, CH])
        rstd_cur = sb("rstd_cur", [P, ROT, CH])
        shift_cur = sb("shift_cur", [P, ROT, CH])
        bias0 = sb("bias0", [P, 1])
        lbias = sb("lbias", [P, ROT])
        smax = sb("smax", [P, ROT, SB])
        nmax = sb("nmax", [P, ROT])
        esum = sb("esum", [P, ROT, SB])
        esum1 = sb("esum1", [P, ROT])
        einv = sb("einv", [P, ROT])
        tsum = sb("tsum", [P, 4])
        tsum_e = sb("tsum_e", [P, 4])
        tinv = sb("tinv", [P, 4])
        mrow = sb("mrow", [1, K])
        mcol = sb("mcol", [P, 1])
        omean = sb("omean", [P, CH])
        bn_s = sb("bn_s", [P, CH])
        bn_d = sb("bn_d", [P, CH])
        bn_m = sb("bn_m", [P, CH])
        bn_t = sb("bn_t", [P, CH])
        gstd = sb("gstd", [P, B, CH])
        coef = sb("coef", [P, B, CH])
        Tcol = sb("Tcol", [P, B, CH])
        cur = sb("cur", [P, 3, 3, CH])

        with ExitStack() as first:
            def sb1(name, shape, dt=F32):
                return first.enter_context(nc.sbuf_tensor(name, shape, dt))

            soft = sb1("soft", [P, SOFT, ST])
            x_hl = sb1("x_hl", [P, 3, 2, XSPLIT, ST], F32R)
            A_hl = sb1("A_hl", [P, ROT, 2, XSPLIT, K], F32R)
        attn2 = sb("attn2", [P, A2_SLOTS, 4 * K])
        attnT_hi = sb("attnT_hi", [P, 2, ST], F32R)
        attnT_lo = sb("attnT_lo", [P, 2, ST], F32R)
        Wout_hi = sb("Wout_hi", [P, 3, C], F32R)
        Wout_lo = sb("Wout_lo", [P, 3, C], F32R)
        MvC = sb("MvC", [P, CH, K])
        MvS = sb("MvS", [P, CH, K])

        xs = stage[:, :, :].rearrange("p s (j c) -> p s j c", j=4)
        zs = stage[:, 0:2, :].rearrange("p s (c n) -> p s c n", c=CH)
        prod = stage[:, 2, 0:C]
        gram, gram_hl, gram_hh, gram_half, cov = (stage[:, 2, C + i * K:C + (i + 1) * K] for i in range(5))
        MvS0 = ring[:, 9, 0:C].rearrange("p (c k) -> p c k", c=CH)
        WqS = ring[:, 10, :].rearrange("p (d c) -> p d c", d=CH)
        MkS = ring[:, 11, 0:C]
        MkT = ring[:, 11, 2 * C:3 * C].rearrange("p (d k) -> p d k", d=CH)

        ps = ctx.enter_context(nc.psum_tensor("ps", [P, 8, 512], F32))
        xtb = ps[:, 0:4, :]
        logit_b = ps[:, 4, :]
        turn_b = ps[:, 5, :]
        gram_b = ps[:, 6, 0:2 * K]
        misc = ps[:, 7, :]
        q_b = ps[:, 0:3, :]
        back_b = ps[:, 3:7, :]
        turn2_b = ps[:, 7, :]

        ident_zeroed = sem("ident_zeroed")
        consts_ready = sem("consts_ready")
        gavg_lower = sem("gavg_lower")
        mk_loaded, wq_loaded, mv_loaded, vecs_loaded = (sem(n) for n in ("mk_loaded", "wq_loaded", "mv_loaded", "vecs_loaded"))
        setup_psum = sem("setup_psum")
        setup_sbuf = sem("setup_sbuf")
        x_loaded = [sem(f"x_loaded{i}") for i in range(STAGE)]
        xt_ready = sem("xt_ready")
        xt_copied = sem("xt_copied")
        stats_ready = sem("stats_ready")
        chan_ready = sem("chan_ready")
        gmean_ready = sem("gmean_ready")
        dev_ready = sem("dev_ready")
        dev2_ready = sem("dev2_ready")
        spread_ready = sem("spread_ready")
        gvar_ready = sem("gvar_ready")
        var_e_ready = sem("var_e_ready")
        guess_ready = sem("guess_ready")
        nw1_ready, nw2_ready, nw3_ready = (sem(f"nw{i}_ready") for i in (1, 2, 3))
        rstd_ready = sem("rstd_ready")
        shift_ready = sem("shift_ready")
        weights_scaled = sem("weights_scaled")
        weights_hi = sem("weights_hi")
        weights_ready = sem("weights_ready")
        x_hi_ready = sem("x_hi_ready")
        x_lo_ready = sem("x_lo_ready")
        cols_kept = sem("cols_kept")
        lshift_ready = sem("lshift_ready")
        lbias_ready = sem("lbias_ready")
        logits_ready = sem("logits_ready")
        logits_copied = sem("logits_copied")
        nmax_ready = sem("nmax_ready")
        exp_ready = sem("exp_ready")
        esum_ready = sem("esum_ready")
        einv_ready = sem("einv_ready")
        probs_ready = sem("probs_ready")
        turned = sem("turned")
        tsum_ready = sem("tsum_ready")
        tsum_e_ready = sem("tsum_e_ready")
        tinv_ready = sem("tinv_ready")
        attn_ready = sem("attn_ready")
        attn_hi_ready = sem("attn_hi_ready")
        attn_lo_ready = sem("attn_lo_ready")
        gram_done = sem("gram_done")
        acc_zeroed = sem("acc_zeroed")
        attn_added = sem("attn_added")
        attn_spilled = [sem(f"attn_spilled{i}") for i in range(ATTN_SLOTS)]
        gram_parts = sem("gram_parts")
        gram_turned = sem("gram_turned")
        bn_psum = sem("bn_psum")
        bn_sbuf = sem("bn_sbuf")
        bn_self = sem("bn_self")
        bn_guess = sem("bn_guess")
        x2_loaded = [sem(f"x2_loaded{i}") for i in range(X_SLOTS)]
        y_stored = [sem(f"y_stored{i}") for i in range(X_SLOTS)]
        attn2_loaded = [sem(f"attn2_loaded{i}") for i in range(A2_SLOTS)]
        attnT_ready = sem("attnT_ready")
        attnT_hi_ready = sem("attnT_hi_ready")
        attnT_lo_ready = sem("attnT_lo_ready")
        mv2_loaded = sem("mv2_loaded")
        cur_ready = sem("cur_ready")
        MvS_ready = sem("MvS_ready")
        Wout_psum = sem("Wout_psum")
        Wout_hi_ready = sem("Wout_hi_ready")
        Wout_lo_ready = sem("Wout_lo_ready")
        q_filled = sem("q_filled")
        z_ready = sem("z_ready")
        leaky_done = sem("leaky_done")
        turned_back = sem("turned_back")
        y_ready = sem("y_ready")

        def in_range(k, j, lag, unroll=UNROLL1):
            return not isinstance(k, int) or 0 <= unroll * k + j - lag < NS

        def since(k, j, lag, unroll=UNROLL1):
            n = unroll * k + j - lag
            return None if isinstance(n, int) and n < 0 else n

        def drained(k, j, lag):
            return isinstance(k, int) and NS - DRAIN <= UNROLL1 * k + j - lag < NS

        def probs_on_act(k, j):
            return (j - LAG_EXP) % SB >= 3 or drained(k, j, LAG_PROBS)

        def turn_bank(k, j):
            free = isinstance(k, int) and UNROLL1 * k + j >= NS + 2
            return ps[:, 0, :] if free and j % 2 else turn_b

        def pass1(eng, step):
            last = NS // UNROLL1
            for j in range(UNROLL1):
                step(0, j)
            with eng.Fori(1, last) as k:
                for j in range(UNROLL1):
                    step(k, j)
            for n in range(NS + LAG_SPILL - UNROLL1 * last):
                step(last + n // UNROLL1, n % UNROLL1)

        def pass2(eng, step):
            whole = NS // UNROLL2
            for j in range(UNROLL2):
                step(0, j)
            with eng.Fori(1, whole) as k:
                for j in range(UNROLL2):
                    step(k, j)
            for j in range(NS - whole * UNROLL2):
                step(whole, j)

        def batch(k, j, lag):
            return ROT * k + (j - lag) // SB

        block = ctx.enter_context(nc.Block())

        @block.sync
        def _(sp):
            sp.dma_start(stage[:, 0, :], x_st[0]).then_inc(x_loaded[0], 16)
            sp.dma_start(MkS, Mk).then_inc(mk_loaded, 16)
            for n, v in enumerate((bq, bv, gamma, beta)):
                sp.dma_start(vecs[CH * n:CH * n + CH, :], v.rearrange("(c p) -> c p", p=P)).then_inc(vecs_loaded, 16)
            sp.dma_start(MvS0, Mv.rearrange("(c p) k -> p c k", p=P)).then_inc(mv_loaded, 16)
            for i in range(1, STAGE):
                if i == 2:
                    sp.dma_start(WqS, Wq.rearrange("(d p) c -> p d c", p=P)).then_inc(wq_loaded, 16)
                sp.dma_start(stage[:, i, :], x_st[i]).then_inc(x_loaded[i], 16)

            def step(k, j):
                s = UNROLL1 * k + j
                n, q = since(k, j, LAG_LOAD), (j - LAG_LOAD) % STAGE
                if in_range(k, j, LAG_LOAD) and not (isinstance(k, int) and n < STAGE):
                    sp.wait_ge(xt_ready, 2 * (n - STAGE + 1))
                    sp.dma_start(stage[:, q, :], x_st[n]).then_inc(x_loaded[q], 16)
                if in_range(k, j, LAG_SPILL):
                    n, q = since(k, j, LAG_SPILL), (j - LAG_SPILL) % ATTN_SLOTS
                    sp.wait_ge(attn_ready, n + 1)
                    sp.dma_start(attn_dram[n], attn[:, q, :]).then_inc(attn_spilled[q], 16)
                last = s - LAG_LOGITS - 1
                if isinstance(k, int) and NS - X_SLOTS <= last < NS:
                    sp.wait_ge(logits_ready, last + 1)
                    i = last % X_SLOTS
                    sp.dma_start(ring[:, i, :], x_st[i]).then_inc(x2_loaded[i], 16)

            pass1(sp, step)
            for q, sem_q in enumerate(attn_spilled):
                sp.wait_ge(sem_q, 16 * ((NS - q + ATTN_SLOTS - 1) // ATTN_SLOTS))
            sp.dma_start(MvC[:, :, :], Mv.rearrange("(c p) k -> p c k", p=P)).then_inc(mv2_loaded, 16)
            for i in range(A2_AHEAD):
                sp.dma_start(attn2[:, i, :], attn_dram[i]).then_inc(attn2_loaded[i], 16)

            def step2(k, j):
                i = UNROLL2 * k + j
                static = isinstance(k, int)
                if not static or X_SLOTS <= i + X2_AHEAD < NS:
                    n = X2_AHEAD + j
                    q = n % X_SLOTS
                    sp.wait_ge(y_stored[q], 16 * (2 * k + n // X_SLOTS))
                    sp.dma_start(ring[:, q, :], x_st[i + X2_AHEAD]).then_inc(x2_loaded[q], 16)
                if not static or i + A2_AHEAD < NS:
                    if not static or i >= 1:
                        sp.wait_ge(attnT_ready, i)
                    q = (j + A2_AHEAD) % A2_SLOTS
                    sp.dma_start(attn2[:, q, :], attn_dram[i + A2_AHEAD]).then_inc(attn2_loaded[q], 16)
                sp.wait_ge(y_ready, 2 * i + 2)
                sp.dma_start(y_st[i], ring[:, j % X_SLOTS, :]).then_inc(y_stored[j % X_SLOTS], 16)

            pass2(sp, step2)
            for q in range(X_SLOTS):
                sp.wait_ge(y_stored[q], 16 * ((NS - q + X_SLOTS - 1) // X_SLOTS))

        @block.gpsimd
        def _(pool):
            pool.memset(ident[:, :], 0.0).then_inc(ident_zeroed, 1)
            pool.memset(gavg[:, :], 1.0 / GC).then_inc(ident_zeroed, 1)
            pool.memset(ones[:, :], 1.0).then_inc(consts_ready, 1)
            pool.memset(half_neg[:, :], -0.5).then_inc(consts_ready, 1)
            pool.wait_ge(ident_zeroed, 2)
            pool.affine_select(out=ident[:, :], in_=ident[:, :], compare_op=ALU.not_equal, fill=1.0, base=0,
                               pattern=[[-1, P]], channel_multiplier=1).then_inc(consts_ready, 1)
            gv = gavg[:, :].rearrange("p (g c) -> p g c", c=GC)
            pool.affine_select(out=gv, in_=gv, compare_op=ALU.is_ge, fill=0.0, base=0,
                               pattern=[[-GC, P // GC], [0, GC]], channel_multiplier=1).then_inc(gavg_lower, 1)
            pool.wait_ge(gavg_lower, 1)
            pool.affine_select(out=gv, in_=gv, compare_op=ALU.is_ge, fill=0.0, base=GC - 1,
                               pattern=[[GC, P // GC], [0, GC]], channel_multiplier=-1).then_inc(consts_ready, 1)
            pool.memset(attn_acc[:, :], 0.0).then_inc(acc_zeroed, 1)
            pool.wait_ge(acc_zeroed, 1)

            def step(k, j):
                if j % SB == 1 and in_range(k, j, SB + 1):
                    pool.wait_ge(var_e_ready, batch(k, j, SB + 1) + 1)
                    pool.tensor_tensor(guess[:, :], var_e[:, :], half_neg[:, :], ALU.pow).then_inc(guess_ready, 1)
                if in_range(k, j, LAG_XSPLIT):
                    n, q = since(k, j, LAG_XSPLIT), (j - LAG_XSPLIT) % X_SLOTS
                    pool.wait_ge(x_hi_ready, n + 1)
                    pool.tensor_tensor(x_hl[:, q % 3, 1, :, :].rearrange("p c n -> p (c n)"), ring[:, q, 0:XSPLIT * ST],
                                       x_hl[:, q % 3, 0, :, :].rearrange("p c n -> p (c n)"), ALU.subtract)\
                        .then_inc(x_lo_ready, 1)
                if in_range(k, j, LAG_PROBS) and not probs_on_act(k, j):
                    pool.wait_ge(einv_ready, batch(k, j, LAG_PROBS) + 1)
                    pool.wait_ge(probs_ready, since(k, j, LAG_PROBS))
                if in_range(k, j, LAG_SPLIT):
                    n, q = since(k, j, LAG_SPLIT), (j - LAG_SPLIT) % ATTN_SLOTS

                    def add():
                        if not isinstance(k, int) or n >= 1:
                            pool.wait_ge(attn_added, n)
                        pool.tensor_tensor(attn_acc[:, :], attn_acc[:, :], attn[:, q, :], ALU.add).then_inc(attn_added, 1)

                    def split():
                        pool.wait_ge(attn_hi_ready, n + 1)
                        hl = attn_hl[:, (j - LAG_SPLIT) % 2, :, :, :]
                        pool.tensor_tensor(hl[:, :, 1, :], attn[:, q, :].rearrange("p (t k) -> p t k", t=4),
                                           hl[:, :, 0, :], ALU.subtract).then_inc(attn_lo_ready, 1)

                    pool.wait_ge(attn_ready, n + 1)
                    if not drained(k, j, LAG_SPLIT):
                        add()
                        split()
                    elif j % 2:
                        add()
                    else:
                        pool.wait_ge(attn_lo_ready, n)
                        split()
                        add()
                if in_range(k, j, LAG_PROBS) and not probs_on_act(k, j):
                    q = (j - LAG_PROBS) % SOFT
                    b2 = ((j - LAG_PROBS) // SB) % ROT
                    pool.tensor_scalar(soft[:, q, :], soft[:, q, :], einv[:, b2:b2 + 1], 1.0, ALU.mult,
                                       ALU.mult).then_inc(probs_ready, 1)

            pass1(pool, step)
            pool.wait_ge(bn_sbuf, 5)
            pool.tensor_tensor(guess[:, :], var_e[:, :], half_neg[:, :], ALU.pow).then_inc(bn_guess, 1)

        @block.tensor
        def _(pe):
            pe.wait_ge(consts_ready, 4)

            def setup1():
                pe.wait_ge(mk_loaded, 16)
                for d in range(CH):
                    mm = pe.transpose(misc[:, d * P:(d + 1) * P], MkS[:, d * P:(d + 1) * P], ident[:, :])
                mm.then_inc(setup_psum, 1)
                pe.wait_ge(mv_loaded, 16)
                for c in range(CH):
                    mm = pe.transpose(logit_b[:, c * P:(c + 1) * P], MvS0[:, c, :], ident[:, :])
                mm.then_inc(setup_psum, 1)
                pe.wait_ge(vecs_loaded, 64)
                pe.transpose(turn_b[:, 0:16], vecs[:, :], ident[0:16, 0:16]).then_inc(setup_psum, 1)

            def setup2(c):
                if c == 0:
                    pe.wait_ge(wq_loaded, 16)
                    pe.wait_ge(setup_sbuf, 3)
                for d in range(CH):
                    mm = pe.matmul(turn_b[:, c * K:(c + 1) * K], WqS[:, d, c * P:(c + 1) * P], MkT[:, d, :],
                                   start=(d == 0), stop=(d == CH - 1))
                if c == CH - 1:
                    mm.then_inc(setup_psum, 1)
                    for d in range(CH):
                        mm = pe.matmul(ps[:, 6, 0:1], MkT[:, d, :], vcol[:, 0, d:d + 1], start=(d == 0), stop=(d == CH - 1))
                    mm.then_inc(setup_psum, 1)

            def step(k, j):
                if isinstance(k, int) and UNROLL1 * k + j == 3:
                    setup1()
                if isinstance(k, int) and 5 <= UNROLL1 * k + j < 5 + CH:
                    setup2(UNROLL1 * k + j - 5)
                if isinstance(k, int) and UNROLL1 * k + j == 10:
                    pe.wait_ge(setup_sbuf, 5)
                s = since(k, j, 0)
                if in_range(k, j, 0):
                    pe.wait_ge(x_loaded[j % STAGE], 16 * (UNROLL1 // STAGE * k + j // STAGE + 1))
                    for h in range(2):
                        if not isinstance(k, int) or s >= 1:
                            pe.wait_ge(xt_copied, 2 * s + h - 1)
                        for c in (2 * h, 2 * h + 1):
                            for t in range(4):
                                mm = pe.transpose(xtb[:, c, t * P:(t + 1) * P], xs[:, j % STAGE, t, c * P:(c + 1) * P],
                                                  ident[:, :])
                        mm.then_inc(xt_ready, 1)
                if j % SB == 1 and in_range(k, j, SB + 1):
                    pe.wait_ge(spread_ready, batch(k, j, SB + 1) + 1)
                    pe.matmul(misc[:, 8:8 + CH], gavg[:, :], spread[:, :], start=True, stop=True).then_inc(gvar_ready, 1)
                if j % SB == 2 and in_range(k, j, SB + 2):
                    pe.wait_ge(shift_ready, batch(k, j, SB + 2) + 1)
                    par = ((j - SB - 2) // SB) % ROT
                    for c in range(CH):
                        mm = pe.matmul(misc[:, 16:17], AT[:, c, :], shift_cur[:, par, c:c + 1], start=(c == 0), stop=(c == CH - 1))
                    mm.then_inc(lshift_ready, 1)
                if in_range(k, j, LAG_LOGITS):
                    n, q = since(k, j, LAG_LOGITS), (j - LAG_LOGITS) % X_SLOTS
                    par = ((j - LAG_LOGITS) // SB) % ROT
                    if (j - LAG_LOGITS) % SB == 0:
                        pe.wait_ge(weights_ready, batch(k, j, LAG_LOGITS) + 1)
                    if not isinstance(k, int) or n >= 1:
                        pe.wait_ge(logits_copied, n)
                    for c in range(XSPLIT, CH):
                        pe.matmul(logit_b, ATs[:, par, c, :], ring[:, q, c * ST:(c + 1) * ST],
                                  start=(c == XSPLIT), stop=False, skip_group_check=True)
                    pe.wait_ge(x_lo_ready, n + 1)
                    for c in range(XSPLIT):
                        for w, v in ((0, 0), (0, 1), (1, 0)):
                            mm = pe.matmul(logit_b, A_hl[:, par, w, c, :], x_hl[:, q % 3, v, c, :], start=False,
                                           stop=(c == XSPLIT - 1 and w == 1), skip_group_check=True)
                    mm.then_inc(logits_ready, 1)
                if in_range(k, j, LAG_TURN):
                    n, q = since(k, j, LAG_TURN), (j - LAG_TURN) % SOFT
                    pe.wait_ge(probs_ready, n + 1)
                    if isinstance(k, int) and s == NS + 3:
                        pe.wait_ge(xt_copied, 2 * NS)
                    elif isinstance(k, int) and s > NS + 3:
                        pe.wait_ge(attn_ready, n - 1)
                    elif not isinstance(k, int) or n >= 1:
                        pe.wait_ge(attn_ready, n)
                    for t in range(4):
                        mm = pe.transpose(turn_bank(k, j)[:, t * P:(t + 1) * P], soft[:, q, t * P:(t + 1) * P], ident[:, :])
                    mm.then_inc(turned, 1)
                if in_range(k, j, LAG_GRAM):
                    n, q = since(k, j, LAG_GRAM), (j - LAG_GRAM) % 2
                    pe.wait_ge(attn_lo_ready, n + 1)
                    for t in range(4):
                        mm = pe.matmul(gram_b, attn_hl[:, q, t, 0, :], attn_hl[:, q, t, :, :],
                                       start=(isinstance(k, int) and n == 0 and t == 0),
                                       stop=(isinstance(k, int) and n == NS - 1 and t == 3), skip_group_check=True)
                    mm.then_inc(gram_done, 1)
                if j % SB == 0 and in_range(k, j, SB):
                    pe.wait_ge(chan_ready, batch(k, j, SB) + 1)
                    pe.matmul(misc[:, 0:CH], gavg[:, :], chan[:, :, 0], start=True, stop=True).then_inc(gmean_ready, 1)

            pass1(pe, step)

            pe.wait_ge(gram_parts, 1)
            pe.transpose(turn_b[:, 0:K], gram_hl, ident[:, :]).then_inc(gram_turned, 1)
            pe.wait_ge(attn_added, NS)
            for t in range(4):
                mm = pe.matmul(misc[0:1, 0:K], ones[:, 0:1], attn_acc[:, t * K:(t + 1) * K], start=(t == 0), stop=(t == 3))
            mm.then_inc(bn_psum, 1)
            pe.wait_ge(bn_sbuf, 1)
            pe.matmul(misc[:, 2 * K:3 * K], mrow[:, :], mrow[:, :], start=True, stop=True).then_inc(bn_psum, 1)
            for t in range(4):
                mm = pe.matmul(logit_b[:, 0:1], attn_acc[:, t * K:(t + 1) * K], ones[:, 0:1], start=(t == 0), stop=(t == 3))
            mm.then_inc(bn_psum, 1)
            pe.wait_ge(bn_sbuf, 2)
            pe.matmul(turn_b, cov, MvT[:, :], start=True, stop=True).then_inc(bn_psum, 1)
            pe.wait_ge(bn_sbuf, 3)
            for c in range(CH):
                mm = pe.matmul(logit_b[:, 8 + c:9 + c], MvT[:, c * P:(c + 1) * P], mcol[:, :], start=True, stop=True)
            mm.then_inc(bn_psum, 1)
            pe.wait_ge(bn_sbuf, 4)
            for c in range(CH):
                mm = pe.matmul(misc[:, 3 * K + c:3 * K + c + 1], prod[:, c * P:(c + 1) * P], ones[:, 0:1], start=True, stop=True)
            mm.then_inc(bn_psum, 1)

            def weights(b):
                pe.wait_ge(MvS_ready, b + 1)
                for c in range(CH):
                    mm = pe.transpose(turn2_b[:, c * P:(c + 1) * P], MvS[:, c, :], ident[:, :])
                mm.then_inc(Wout_psum, 1)

            def turn_attn(k, j):
                i = UNROLL2 * k + j
                pe.wait_ge(attn2_loaded[j % A2_SLOTS], 16 * (3 * k + j // A2_SLOTS + 1))
                if j % SB == 5 and (not isinstance(k, int) or i - 2 + SB < NS):
                    pe.wait_ge(Wout_lo_ready, 3 * k + j // SB + 2)
                elif not isinstance(i, int) or i >= 1:
                    pe.wait_ge(attnT_lo_ready, i)
                for t in range(4):
                    mm = pe.transpose(turn2_b[:, t * P:(t + 1) * P], attn2[:, j % A2_SLOTS, t * K:(t + 1) * K], ident[:, :])
                mm.then_inc(attnT_ready, 1)

            weights(0)
            pe.wait_ge(Wout_lo_ready, 1)
            turn_attn(0, 0)

            def turn_back(k, j, h):
                i = UNROLL2 * k + j
                if h == 0:
                    pe.wait_ge(leaky_done, 2 * i + 2)
                if not isinstance(i, int) or i >= 1:
                    pe.wait_ge(y_ready, 2 * i - 1 + h)
                for t in (2 * h, 2 * h + 1):
                    for c in range(CH):
                        mm = pe.transpose(back_b[:, t, c * P:(c + 1) * P], zs[:, j % 2, c, t * P:(t + 1) * P], ident[:, :])
                mm.then_inc(turned_back, 1)

            def step2(k, j):
                i = UNROLL2 * k + j
                static = isinstance(k, int)
                if not static or i + 1 < NS:
                    turn_attn(k, j + 1)
                pe.wait_ge(x2_loaded[j % X_SLOTS], 16 * (2 * k + j // X_SLOTS + 1))
                if j % SB == 0:
                    pe.wait_ge(Wout_lo_ready, 3 * k + j // SB + 1)
                for c in range(CH):
                    m = 4 * j + c
                    if not static or 4 * i + c >= 3:
                        pe.wait_ge(z_ready, 4 * i + c - 2)
                    for t in range(4):
                        xt = ring[:, j % X_SLOTS, t * C + c * P:t * C + (c + 1) * P]
                        pe.matmul(q_b[:, m % 3, t * P:(t + 1) * P], xt, ident[:, :], is_transpose=True,
                                  start=(t == 0), stop=False, skip_group_check=True)
                    if c == 0:
                        pe.wait_ge(attnT_lo_ready, i + 1)
                    W_hi, W_lo = (W[:, j // SB, c * P:(c + 1) * P] for W in (Wout_hi, Wout_lo))
                    pe.matmul(q_b[:, m % 3, :], W_hi, attnT_hi[:, j % 2, :], start=False, stop=False, skip_group_check=True)
                    pe.matmul(q_b[:, m % 3, :], W_hi, attnT_lo[:, j % 2, :], start=False, stop=False, skip_group_check=True)
                    pe.matmul(q_b[:, m % 3, :], W_lo, attnT_hi[:, j % 2, :], start=False, stop=True, skip_group_check=True)\
                      .then_inc(q_filled, 1)
                    if c % 2 and (not static or i >= 1):
                        turn_back(k, j - 1, c // 2)
                    if c == 1 and j % SB == 3 and (not static or i + SB < NS):
                        pe.wait_ge(attnT_lo_ready, i + 2)
                        weights(3 * k + j // SB + 1)

            pass2(pe, step2)
            last = NS - 1
            for h in range(2):
                turn_back(last // UNROLL2, last % UNROLL2, h)

        @block.scalar
        def _(act):
            def step(k, j):
                s = since(k, j, 0)
                if in_range(k, j, LAG_XSPLIT):
                    n, q = since(k, j, LAG_XSPLIT), (j - LAG_XSPLIT) % X_SLOTS
                    if not isinstance(k, int) or n >= 3:
                        act.wait_ge(logits_ready, n - 2)
                    act.activation(x_hl[:, q % 3, 0, :, :].rearrange("p c n -> p (c n)"), ring[:, q, 0:XSPLIT * ST],
                                   ACT.Copy).then_inc(x_hi_ready, 1)
                if in_range(k, j, 0):
                    if not isinstance(k, int) or s >= X_SLOTS:
                        act.wait_ge(logits_ready, s - X_SLOTS + 1)
                    for h in range(2):
                        act.wait_ge(xt_ready, 2 * s + h + 1)
                        act.activation(ring[:, j % X_SLOTS, 2 * h * ST:2 * (h + 1) * ST].rearrange("p (c n) -> p c n", c=2),
                                       xtb[:, 2 * h:2 * h + 2, :], ACT.Copy).then_inc(xt_copied, 1)
                g = (j - LAG_EXP) % SB
                if g < 3 and in_range(k, j, LAG_EXP):
                    b, par = batch(k, j, LAG_EXP), ((j - LAG_EXP) // SB) % ROT
                    if g == 0:
                        act.wait_ge(nmax_ready, b + 1)
                    for e in range(3 * g, min(3 * g + 3, SB)):
                        q = (SB * ((j - LAG_EXP) // SB) + e) % SOFT
                        act.activation(soft[:, q, :], soft[:, q, :], ACT.Exp, bias=nmax[:, par:par + 1],
                                       accum_out=esum[:, par, e:e + 1]).then_inc(exp_ready, 1)
                if in_range(k, j, LAG_SPLIT):
                    n, q = since(k, j, LAG_SPLIT), (j - LAG_SPLIT) % ATTN_SLOTS
                    act.wait_ge(attn_ready, n + 1)
                    if not isinstance(k, int) or n >= 2:
                        act.wait_ge(gram_done, n - 1)
                    act.activation(attn_hl[:, (j - LAG_SPLIT) % 2, :, 0, :], attn[:, q, :].rearrange("p (t k) -> p t k", t=4),
                                   ACT.Copy).then_inc(attn_hi_ready, 1)
                if in_range(k, j, LAG_PROBS) and probs_on_act(k, j):
                    n, q = since(k, j, LAG_PROBS), (j - LAG_PROBS) % SOFT
                    b2 = ((j - LAG_PROBS) // SB) % ROT
                    act.wait_ge(einv_ready, batch(k, j, LAG_PROBS) + 1)
                    if not isinstance(k, int) or n >= 1:
                        act.wait_ge(probs_ready, n)
                    act.activation(soft[:, q, :], soft[:, q, :], ACT.Identity, scale=einv[:, b2:b2 + 1])\
                       .then_inc(probs_ready, 1)
            pass1(act, step)

            def copy_weights(b, b3):
                act.wait_ge(Wout_psum, b + 1)
                act.activation(Wout_hi[:, b3, :], turn2_b, ACT.Copy).then_inc(Wout_hi_ready, 1)

            def copy_attnT(k, j):
                i = UNROLL2 * k + j
                act.wait_ge(attnT_ready, i + 1)
                if not isinstance(i, int) or i >= 2:
                    act.wait_ge(q_filled, 4 * i - 4)
                act.activation(attnT_hi[:, j % 2, :], turn2_b, ACT.Copy).then_inc(attnT_hi_ready, 1)

            copy_weights(0, 0)
            copy_attnT(0, 0)

            def step2(k, j):
                i = UNROLL2 * k + j
                static = isinstance(k, int)
                if not static or i + 1 < NS:
                    copy_attnT(k, j + 1)
                b3 = j // SB
                for c in range(CH):
                    act.wait_ge(q_filled, 4 * i + c + 1)
                    if c == 0 and (not static or i >= 2):
                        act.wait_ge(turned_back, 2 * i - 2)
                    act.activation(zs[:, j % 2, c, :], q_b[:, (4 * j + c) % 3, :], ACT.Identity,
                                   bias=cur[:, b3, 1, c:c + 1], scale=cur[:, b3, 0, c:c + 1]).then_inc(z_ready, 1)
                    if c == 1 and j % SB == 3 and (not static or i + SB < NS):
                        copy_weights(3 * k + b3 + 1, (b3 + 1) % 3)

            pass2(act, step2)

        @block.vector
        def _(dve):
            dve.wait_ge(consts_ready, 4)

            def setup1():
                dve.wait_ge(setup_psum, 1)
                dve.tensor_copy(ring[:, 11, 2 * C:3 * C], misc).then_inc(setup_sbuf, 1)
                dve.wait_ge(setup_psum, 2)
                dve.tensor_copy(MvT[:, :], logit_b).then_inc(setup_sbuf, 1)
                dve.wait_ge(setup_psum, 3)
                dve.tensor_copy(vcol[:, :, :].rearrange("p v c -> p (v c)"), turn_b[:, 0:16]).then_inc(setup_sbuf, 1)

            def setup2():
                dve.wait_ge(setup_psum, 4)
                dve.tensor_copy(AT[:, :, :].rearrange("p c k -> p (c k)"), turn_b).then_inc(setup_sbuf, 1)
                dve.wait_ge(setup_psum, 5)
                dve.tensor_copy(bias0[:, :], ps[:, 6, 0:1]).then_inc(setup_sbuf, 1)
                dve.wait_ge(setup_sbuf, 5)

            def newton(n, done):
                dve.tensor_tensor(nw1[:, :], guess[:, :], guess[:, :], ALU.mult).then_inc(nw1_ready, 1)
                dve.wait_ge(nw1_ready, n)
                dve.tensor_tensor(nw2[:, :], nw1[:, :], var_e[:, :], ALU.mult).then_inc(nw2_ready, 1)
                dve.wait_ge(nw2_ready, n)
                dve.tensor_scalar(nw3[:, :], nw2[:, :], -0.5, 1.5, ALU.mult, ALU.add).then_inc(nw3_ready, 1)
                dve.wait_ge(nw3_ready, n)
                dve.tensor_tensor(done, guess[:, :], nw3[:, :], ALU.mult).then_inc(rstd_ready, 1)
                dve.wait_ge(rstd_ready, n)

            def step(k, j):
                static = isinstance(k, int)
                if static and UNROLL1 * k + j == 4:
                    setup1()
                if static and UNROLL1 * k + j == 9:
                    setup2()
                s = since(k, j, 0)
                complete = j % SB == 0 and in_range(k, j, SB)
                if complete:
                    dve.wait_ge(stats_ready, s)

                def aggregate():
                    par = ((j - SB) // SB) % ROT
                    for c in range(CH):
                        ins = dve.bn_aggr(chan[:, c, :], bnst[:, par, c, :, :].rearrange("p g f -> p (g f)"))
                    ins.then_inc(chan_ready, 1)

                def variance():
                    if j % SB == 1 and in_range(k, j, SB + 1):
                        dve.wait_ge(gvar_ready, batch(k, j, SB + 1) + 1)
                        dve.tensor_scalar(var_e[:, :], misc[:, 8:8 + CH], EPS_GN, None, ALU.add).then_inc(var_e_ready, 1)

                if in_range(k, j, 0):
                    for h in range(2):
                        dve.wait_ge(xt_copied, 2 * s + h + 1)
                        for c in (2 * h, 2 * h + 1):
                            ins = dve.bn_stats(bnst[:, j // SB, c, j % SB, :], ring[:, j % X_SLOTS, c * ST:(c + 1) * ST])
                            if complete and c == 0:
                                aggregate()
                        if h == 0:
                            variance()
                    ins.then_inc(stats_ready, 1)
                else:
                    if complete:
                        aggregate()
                    variance()
                if j % SB == 1 and in_range(k, j, SB + 1):
                    b, par = batch(k, j, SB + 1), ((j - SB - 1) // SB) % ROT
                    dve.wait_ge(var_e_ready, b + 1)
                    dve.wait_ge(guess_ready, b + 1)
                    newton(b + 1, rstd_cur[:, par, :])
                    dve.tensor_tensor(shift_cur[:, par, :], misc[:, 0:CH], rstd_cur[:, par, :], ALU.mult)\
                       .then_inc(shift_ready, 1)
                    dve.tensor_tensor(ATs[:, par, :, :], AT[:, :, :],
                                      rstd_cur[:, par, :].unsqueeze(2).to_broadcast([P, CH, K]),
                                      ALU.mult).then_inc(weights_scaled, 1)
                    dve.wait_ge(weights_scaled, b + 1)
                    dve.tensor_copy(A_hl[:, par, 0, :, :], ATs[:, par, 0:XSPLIT, :]).then_inc(weights_hi, 1)
                    dve.wait_ge(weights_hi, b + 1)
                    dve.tensor_tensor(A_hl[:, par, 1, :, :], ATs[:, par, 0:XSPLIT, :], A_hl[:, par, 0, :, :],
                                      ALU.subtract).then_inc(weights_ready, 1)
                    dve.wait_ge(shift_ready, b + 1)
                    dve.tensor_copy(rstd[:, bass.ds(b, 1), :], rstd_cur[:, par:par + 1, :])
                    dve.tensor_tensor(gstd[:, bass.ds(b, 1), :], var_e[:, :].unsqueeze(1), rstd_cur[:, par:par + 1, :],
                                      ALU.mult)
                    dve.tensor_copy(shift[:, bass.ds(b, 1), :], shift_cur[:, par:par + 1, :]).then_inc(cols_kept, 1)
                if j % SB == 2 and in_range(k, j, SB + 2):
                    b1, par1 = batch(k, j, SB + 2), ((j - SB - 2) // SB) % ROT
                    dve.wait_ge(lshift_ready, b1 + 1)
                    dve.tensor_tensor(lbias[:, par1:par1 + 1], bias0[:, :], misc[:, 16:17], ALU.subtract)\
                       .then_inc(lbias_ready, 1)
                if (j - LAG_PROBS) % SB == 0 and in_range(k, j, LAG_PROBS):
                    bp, parp = batch(k, j, LAG_PROBS), ((j - LAG_PROBS) // SB) % ROT
                    dve.wait_ge(exp_ready, SB * (bp + 1))
                    dve.tensor_reduce(esum1[:, parp:parp + 1], esum[:, parp, :], AX.X, ALU.add).then_inc(esum_ready, 1)
                    dve.wait_ge(esum_ready, bp + 1)
                    dve.reciprocal(einv[:, parp:parp + 1], esum1[:, parp:parp + 1]).then_inc(einv_ready, 1)
                if in_range(k, j, LAG_LOGITS):
                    n, q = since(k, j, LAG_LOGITS), (j - LAG_LOGITS) % SOFT
                    g, parl = (j - LAG_LOGITS) % SB, ((j - LAG_LOGITS) // SB) % ROT
                    bl = batch(k, j, LAG_LOGITS)
                    dve.wait_ge(lbias_ready, bl + 1)
                    dve.wait_ge(logits_ready, n + 1)
                    if not static or n >= SOFT:
                        dve.wait_ge(turned, n - SOFT + 1)
                    dve.tensor_scalar(soft[:, q, :], logit_b, lbias[:, parl:parl + 1], None, ALU.add, ALU.max,
                                      accum_out=smax[:, parl, g:g + 1]).then_inc(logits_copied, 1)
                    if g == SB - 1:
                        dve.wait_ge(logits_copied, n + 1)
                        dve.tensor_reduce(nmax[:, parl:parl + 1], smax[:, parl, :], AX.X, ALU.max, negate=True)\
                           .then_inc(nmax_ready, 1)
                if in_range(k, j, LAG_TURN):
                    n, q = since(k, j, LAG_TURN), (j - LAG_TURN) % ATTN_SLOTS
                    tb = turn_bank(k, j).rearrange("p (t k) -> p t k", t=4)
                    dve.wait_ge(turned, n + 1)
                    dve.tensor_reduce(tsum[:, :], tb, AX.X, ALU.add).then_inc(tsum_ready, 1)
                    dve.wait_ge(tsum_ready, n + 1)
                    dve.tensor_scalar(tsum_e[:, :], tsum[:, :], EPS_L1, None, ALU.add).then_inc(tsum_e_ready, 1)
                    dve.wait_ge(tsum_e_ready, n + 1)
                    dve.reciprocal(tinv[:, :], tsum_e[:, :]).then_inc(tinv_ready, 1)
                    dve.wait_ge(tinv_ready, n + 1)
                    if not static or n >= ATTN_SLOTS:
                        dve.wait_ge(attn_spilled[q], 16 * (UNROLL1 // ATTN_SLOTS * k + (j - LAG_TURN) // ATTN_SLOTS))
                        dve.wait_ge(attn_added, n - ATTN_SLOTS + 1)
                        dve.wait_ge(attn_lo_ready, n - ATTN_SLOTS + 1)
                    dve.tensor_tensor(attn[:, q, :].rearrange("p (t k) -> p t k", t=4), tb,
                                      tinv[:, :].unsqueeze(2).to_broadcast([P, 4, K]), ALU.mult).then_inc(attn_ready, 1)
                if complete:
                    b = batch(k, j, SB)
                    dve.wait_ge(gmean_ready, b + 1)
                    dve.tensor_tensor(dev[:, :], chan[:, :, 0], misc[:, 0:CH], ALU.subtract).then_inc(dev_ready, 1)
                    dve.wait_ge(dev_ready, b + 1)
                    dve.tensor_tensor(dev2[:, :], dev[:, :], dev[:, :], ALU.mult).then_inc(dev2_ready, 1)
                    dve.wait_ge(dev2_ready, b + 1)
                    dve.tensor_tensor(spread[:, :], dev2[:, :], chan[:, :, 1], ALU.add).then_inc(spread_ready, 1)
                if drained(k, j, LAG_SPLIT) and j % 2:
                    n, q = since(k, j, LAG_SPLIT), (j - LAG_SPLIT) % ATTN_SLOTS
                    dve.wait_ge(attn_lo_ready, n)
                    dve.wait_ge(attn_hi_ready, n + 1)
                    hl = attn_hl[:, (j - LAG_SPLIT) % 2, :, :, :]
                    dve.tensor_tensor(hl[:, :, 1, :], attn[:, q, :].rearrange("p (t k) -> p t k", t=4),
                                      hl[:, :, 0, :], ALU.subtract).then_inc(attn_lo_ready, 1)

            pass1(dve, step)

            dve.wait_ge(gram_done, NS)
            dve.tensor_scalar(gram_hl, gram_b[:, K:2 * K], 1.0 / NTOK, None, ALU.mult).then_inc(gram_parts, 1)
            dve.tensor_scalar(gram_hh, gram_b[:, 0:K], 1.0 / NTOK, None, ALU.mult).then_inc(gram_parts, 1)
            dve.wait_ge(gram_parts, 2)
            dve.tensor_tensor(gram_half, gram_hh, gram_hl, ALU.add).then_inc(gram_parts, 1)
            dve.wait_ge(gram_parts, 3)
            dve.wait_ge(gram_turned, 1)
            dve.tensor_tensor(gram, gram_half, turn_b[:, 0:K], ALU.add).then_inc(gram_parts, 1)
            dve.wait_ge(gram_parts, 4)
            dve.wait_ge(bn_psum, 1)
            dve.tensor_scalar(mrow[:, :], misc[0:1, 0:K], 1.0 / NTOK, None, ALU.mult).then_inc(bn_sbuf, 1)
            dve.wait_ge(bn_psum, 2)
            dve.tensor_tensor(cov, gram, misc[:, 2 * K:3 * K], ALU.subtract).then_inc(bn_sbuf, 1)
            dve.wait_ge(bn_psum, 3)
            dve.tensor_scalar(mcol[:, :], logit_b[:, 0:1], 1.0 / NTOK, None, ALU.mult).then_inc(bn_sbuf, 1)
            dve.wait_ge(bn_psum, 4)
            dve.tensor_tensor(prod, turn_b, MvT[:, :], ALU.mult).then_inc(bn_sbuf, 1)
            dve.wait_ge(bn_psum, 5)
            dve.tensor_tensor(omean[:, :], logit_b[:, 8:8 + CH], vcol[:, 1, :], ALU.add).then_inc(bn_self, 1)
            dve.wait_ge(bn_self, 1)
            dve.tensor_tensor(bn_d[:, :], vcol[:, 1, :], omean[:, :], ALU.subtract).then_inc(bn_self, 1)
            dve.wait_ge(bn_psum, 6)
            dve.tensor_scalar(var_e[:, :], misc[:, 3 * K:3 * K + CH], EPS_BN, None, ALU.add).then_inc(bn_sbuf, 1)
            dve.wait_ge(bn_sbuf, 5)
            dve.wait_ge(bn_guess, 1)
            newton(B + 1, bn_m[:, :])
            dve.tensor_tensor(bn_s[:, :], bn_m[:, :], vcol[:, 2, :], ALU.mult).then_inc(bn_sbuf, 1)
            dve.wait_ge(bn_sbuf, 6)
            dve.wait_ge(bn_self, 2)
            dve.tensor_tensor(dev[:, :], bn_d[:, :], bn_s[:, :], ALU.mult).then_inc(bn_self, 1)
            dve.tensor_tensor(coef[:, :, :], bn_s[:, :].unsqueeze(1).to_broadcast([P, B, CH]), gstd[:, :, :],
                              ALU.mult).then_inc(bn_self, 1)
            dve.wait_ge(bn_self, 4)
            dve.tensor_tensor(bn_t[:, :], dev[:, :], vcol[:, 3, :], ALU.add).then_inc(bn_self, 1)
            dve.wait_ge(bn_self, 5)
            dve.wait_ge(cols_kept, B)
            dve.tensor_tensor(Tcol[:, :, :], bn_t[:, :].unsqueeze(1).to_broadcast([P, B, CH]), shift[:, :, :],
                              ALU.subtract).then_inc(bn_self, 1)
            dve.wait_ge(bn_self, 6)

            def columns(b, b3):
                dve.tensor_copy(cur[:, b3, 0:1, :], rstd[:, bass.ds(b, 1), :])
                dve.tensor_copy(cur[:, b3, 1:2, :], Tcol[:, bass.ds(b, 1), :])
                dve.tensor_copy(cur[:, b3, 2:3, :], coef[:, bass.ds(b, 1), :]).then_inc(cur_ready, 1)
                dve.wait_ge(cur_ready, b + 1)
                dve.wait_ge(mv2_loaded, 16)
                if not isinstance(b, int) or b >= 1:
                    dve.wait_ge(Wout_psum, b)
                dve.tensor_tensor(MvS[:, :, :], MvC[:, :, :], cur[:, b3, 2, :].unsqueeze(2).to_broadcast([P, CH, K]),
                                  ALU.mult).then_inc(MvS_ready, 1)

            def split_weights(b, b3):
                dve.wait_ge(Wout_hi_ready, b + 1)
                dve.tensor_tensor(Wout_lo[:, b3, :], turn2_b, Wout_hi[:, b3, :], ALU.subtract).then_inc(Wout_lo_ready, 1)

            def split_attn(k, j):
                dve.wait_ge(attnT_hi_ready, UNROLL2 * k + j + 1)
                dve.tensor_tensor(attnT_lo[:, j % 2, :], turn2_b, attnT_hi[:, j % 2, :], ALU.subtract)\
                   .then_inc(attnT_lo_ready, 1)

            columns(0, 0)
            split_weights(0, 0)
            split_attn(0, 0)

            def finish(k, j, h):
                xh = ring[:, j % X_SLOTS, 2 * h * C:2 * (h + 1) * C].rearrange("p (t c) -> p t c", t=2)
                dve.wait_ge(turned_back, 2 * (UNROLL2 * k + j) + h + 1)
                dve.tensor_tensor(xh, back_b[:, 2 * h:2 * h + 2, :], xh, ALU.add).then_inc(y_ready, 1)

            def step2(k, j):
                i = UNROLL2 * k + j
                static = isinstance(k, int)
                if not static or i + 1 < NS:
                    split_attn(k, j + 1)
                if j % SB == 2 and (not static or i + SB < NS):
                    columns(3 * k + j // SB + 1, (j // SB + 1) % 3)
                for h in range(2):
                    z = zs[:, j % 2, 2 * h:2 * h + 2, :]
                    dve.wait_ge(z_ready, 4 * i + 2 * h + 2)
                    dve.scalar_tensor_tensor(out=z, in0=z, scalar=LEAK, in1=z, op0=ALU.mult, op1=ALU.max)\
                       .then_inc(leaky_done, 1)
                    if not static or i >= 1:
                        finish(k, j - 1, h)
                    if h == 0 and j % SB == 3 and (not static or i + SB < NS):
                        split_weights(3 * k + j // SB + 1, (j // SB + 1) % 3)

            pass2(dve, step2)
            last = NS - 1
            for h in range(2):
                finish(last // UNROLL2, last % UNROLL2, h)


_INS = ["x", "L0_conv_Wq", "L0_conv_bq", "L0_conv_Mk", "L0_conv_Mv", "L0_conv_bv", "L0_conv_gamma", "L0_conv_beta"]


def kernel(**inputs):
    import numpy as _np
    import concourse.bacc as _bacc
    from concourse import mybir as _mybir
    from concourse.bass_utils import run_bass_kernel_spmd as _run

    nc = _bacc.Bacc("TRN2", target_bir_lowering=False, num_devices=1)
    arrays, args = {}, []
    for name in _INS:
        a = _np.ascontiguousarray(inputs[name])
        arrays[f"in_{name}_dram"] = a
        args.append(nc.dram_tensor(f"in_{name}_dram", a.shape, _mybir.dt.from_np(a.dtype), kind="ExternalInput").ap())
    shape = inputs["x"].shape
    args.append(nc.dram_tensor("out_0_dram", shape, _mybir.dt.float32, kind="ExternalOutput").ap())
    gated_attention_kernel(nc, *args)
    r = _run(nc, [arrays], core_ids=[0])
    return r.results[0]["out_0_dram"]
```
